# Optimizing a Trainium2 kernel written in Bass

```python
import numpy as np
import jax
import jax.numpy as jnp

def _softmax(x, axis=-1):
    return jax.nn.softmax(x, axis=axis)

def _gelu(x):
    return jax.nn.gelu(x, approximate=True)

def _silu(x):
    return jax.nn.silu(x)

def _sigmoid(x):
    return jax.nn.sigmoid(x)

def _layernorm(x, axis=-1, eps=1e-05):
    m = jnp.mean(x, axis=axis, keepdims=True)
    v = jnp.var(x, axis=axis, keepdims=True)
    return (x - m) / jnp.sqrt(v + eps)

def _scatter_add(tgt, idx, src, axis=0):
    return tgt.at[idx].add(src)

def _segment_sum(src, seg, n):
    return jax.ops.segment_sum(src, seg, n)
kernel_name = 'mk_conv_preact_d2_conv_nchw512_r2_0f2770'

def setup_inputs(seed: int=0):
    np.random.seed(seed)
    _w = jnp.asarray

    def _rec_inputs():
        import jax
        import jax.numpy as jnp
        _gk = jax.random.key(seed)
        x = -0.0002928 + 1 * jax.random.normal(jax.random.fold_in(_gk, 1), (2, 256, 32, 32), jnp.float32)
        return x
    x = _rec_inputs()

    def _L0_conv_setup():
        import jax, jax.numpy as jnp
        import numpy as np
        DIM, D_STATE, EXPAND, D_CONV = (256, 16, 2, 4)
        D_INNER = EXPAND * DIM
        DT_RANK = (DIM + 15) // 16
        EPS = 1e-05

        def _clamp(x):
            return jnp.clip(x, -10.0, 10.0)

        def _layernorm(x, w, b):
            mu = x.mean(-1, keepdims=True)
            var = x.var(-1, keepdims=True)
            return (x - mu) * jax.lax.rsqrt(var + EPS) * w + b
        key = jax.random.key(seed)
        ks = jax.random.split(key, 8)
        B, H, W = (2, 32, 32)

        def rn(k, shape, s=0.02):
            return jax.random.normal(k, shape, jnp.float32) * s
        return {'x': jax.random.normal(ks[0], (B, DIM, H, W), jnp.float32), 'norm_w': jnp.ones((DIM,), jnp.float32), 'norm_b': jnp.zeros((DIM,), jnp.float32), 'in_proj_w': rn(ks[1], (2 * D_INNER, DIM)), 'conv_w': rn(ks[2], (D_INNER, 1, D_CONV), 0.1), 'conv_b': jnp.zeros((D_INNER,), jnp.float32), 'x_proj_w': rn(ks[3], (DT_RANK + 2 * D_STATE, D_INNER)), 'dt_proj_w': rn(ks[4], (D_INNER, DT_RANK), 0.1), 'dt_proj_b': jnp.log(jnp.expm1(jnp.full((D_INNER,), 0.01, jnp.float32))), 'A_log': jnp.log(jnp.broadcast_to(jnp.arange(1, D_STATE + 1, dtype=jnp.float32), (D_INNER, D_STATE))), 'D': jnp.ones((D_INNER,), jnp.float32), 'out_proj_w': rn(ks[5], (DIM, D_INNER))}
    _L0_conv_all = _L0_conv_setup()
    _L0_conv_in = {k: v for k, v in _L0_conv_all.items() if k in ('norm_w', 'norm_b', 'in_proj_w', 'conv_w', 'conv_b', 'x_proj_w', 'dt_proj_w', 'dt_proj_b', 'A_log', 'D', 'out_proj_w')}
    del _L0_conv_all

    def _L1_conv_setup():
        import jax, jax.numpy as jnp
        import numpy as np
        DIM = 8
        HEADS = 32
        TOTAL = HEADS * DIM
        QKV_C = 3 * TOTAL
        PW_GROUPS = 3 * HEADS
        GSZ = QKV_C // PW_GROUPS
        EPS_ATT = 1e-15
        EPS_BN = 1e-05

        def _forward(x, qkv_w, dw_w, pw_w, proj_w, bn_gamma, bn_beta, bn_mean, bn_var):
            B, _, H, W = x.shape
            qkv = jnp.einsum('bchw,oc->bohw', x, qkv_w)
            agg = jax.lax.conv_general_dilated(qkv, dw_w, window_strides=(1, 1), padding=((2, 2), (2, 2)), feature_group_count=QKV_C, dimension_numbers=('NCHW', 'OIHW', 'NCHW'))
            agg = agg.reshape(B, PW_GROUPS, GSZ, H, W)
            agg = jnp.einsum('bgihw,goi->bgohw', agg, pw_w).reshape(B, QKV_C, H, W)
            qkv_cat = jnp.concatenate([qkv, agg], axis=1)
            N = H * W
            t = qkv_cat.reshape(B, -1, 3 * DIM, N)
            q = jax.nn.relu(t[:, :, :DIM])
            k = jax.nn.relu(t[:, :, DIM:2 * DIM])
            v = t[:, :, 2 * DIM:]
            v = jnp.concatenate([v, jnp.ones_like(v[:, :, :1])], axis=2)
            vk = jnp.einsum('bhdn,bhen->bhde', v, k)
            out = jnp.einsum('bhde,bhen->bhdn', vk, q)
            out = out[:, :, :-1] / (out[:, :, -1:] + EPS_ATT)
            out = out.reshape(B, -1, H, W)
            out = jnp.einsum('bchw,oc->bohw', out, proj_w)
            inv = bn_gamma / jnp.sqrt(bn_var + EPS_BN)
            out = out * inv[None, :, None, None] + (bn_beta - bn_mean * inv)[None, :, None, None]
            return out
        key = jax.random.key(seed)
        ks = jax.random.split(key, 10)
        B, C, H, W = (8, 256, 32, 32)
        OUT_C = 256
        x = jax.random.normal(ks[0], (B, C, H, W), dtype=jnp.float32)
        qkv_w = jax.random.normal(ks[1], (QKV_C, C), dtype=jnp.float32) * 0.02
        dw_w = jax.random.normal(ks[2], (QKV_C, 1, 5, 5), dtype=jnp.float32) * 0.05
        pw_w = jax.random.normal(ks[3], (PW_GROUPS, GSZ, GSZ), dtype=jnp.float32) * 0.1
        proj_w = jax.random.normal(ks[4], (OUT_C, 2 * TOTAL), dtype=jnp.float32) * 0.02
        bn_gamma = jnp.ones((OUT_C,), jnp.float32)
        bn_beta = jnp.zeros((OUT_C,), jnp.float32)
        bn_mean = jax.random.normal(ks[5], (OUT_C,), dtype=jnp.float32) * 0.01
        bn_var = jax.random.uniform(ks[6], (OUT_C,), minval=0.5, maxval=1.5, dtype=jnp.float32)
        return {'x': x, 'qkv_w': qkv_w, 'dw_w': dw_w, 'pw_w': pw_w, 'proj_w': proj_w, 'bn_gamma': bn_gamma, 'bn_beta': bn_beta, 'bn_mean': bn_mean, 'bn_var': bn_var}
    _L1_conv_all = _L1_conv_setup()
    _L1_conv_in = {k: v for k, v in _L1_conv_all.items() if k in ('qkv_w', 'dw_w', 'pw_w', 'proj_w', 'bn_gamma', 'bn_beta', 'bn_mean', 'bn_var')}
    del _L1_conv_all
    return {'x': x, 'L0_conv_norm_w': _L0_conv_in['norm_w'], 'L0_conv_norm_b': _L0_conv_in['norm_b'], 'L0_conv_in_proj_w': _L0_conv_in['in_proj_w'], 'L0_conv_conv_w': _L0_conv_in['conv_w'], 'L0_conv_conv_b': _L0_conv_in['conv_b'], 'L0_conv_x_proj_w': _L0_conv_in['x_proj_w'], 'L0_conv_dt_proj_w': _L0_conv_in['dt_proj_w'], 'L0_conv_dt_proj_b': _L0_conv_in['dt_proj_b'], 'L0_conv_A_log': _L0_conv_in['A_log'], 'L0_conv_D': _L0_conv_in['D'], 'L0_conv_out_proj_w': _L0_conv_in['out_proj_w'], 'L1_conv_qkv_w': _L1_conv_in['qkv_w'], 'L1_conv_dw_w': _L1_conv_in['dw_w'], 'L1_conv_pw_w': _L1_conv_in['pw_w'], 'L1_conv_proj_w': _L1_conv_in['proj_w'], 'L1_conv_bn_gamma': _L1_conv_in['bn_gamma'], 'L1_conv_bn_beta': _L1_conv_in['bn_beta'], 'L1_conv_bn_mean': _L1_conv_in['bn_mean'], 'L1_conv_bn_var': _L1_conv_in['bn_var']}

def reference(x, L0_conv_norm_w, L0_conv_norm_b, L0_conv_in_proj_w, L0_conv_conv_w, L0_conv_conv_b, L0_conv_x_proj_w, L0_conv_dt_proj_w, L0_conv_dt_proj_b, L0_conv_A_log, L0_conv_D, L0_conv_out_proj_w, L1_conv_qkv_w, L1_conv_dw_w, L1_conv_pw_w, L1_conv_proj_w, L1_conv_bn_gamma, L1_conv_bn_beta, L1_conv_bn_mean, L1_conv_bn_var):
    import jax
    import jax.numpy as jnp

    def _L0_conv_ref(x, norm_w, norm_b, in_proj_w, conv_w, conv_b, x_proj_w, dt_proj_w, dt_proj_b, A_log, D, out_proj_w):
        import jax, jax.numpy as jnp
        import numpy as np
        DIM, D_STATE, EXPAND, D_CONV = (256, 16, 2, 4)
        D_INNER = EXPAND * DIM
        DT_RANK = (DIM + 15) // 16
        EPS = 1e-05

        def _clamp(x):
            return jnp.clip(x, -10.0, 10.0)

        def _layernorm(x, w, b):
            mu = x.mean(-1, keepdims=True)
            var = x.var(-1, keepdims=True)
            return (x - mu) * jax.lax.rsqrt(var + EPS) * w + b
        B, C, H, W = x.shape
        L = H * W
        x = _clamp(x)
        xs = x.reshape(B, C, L).transpose(0, 2, 1)
        xs = _clamp(_layernorm(xs, norm_w, norm_b))
        xz = xs @ in_proj_w.T
        xin, z = jnp.split(xz, 2, axis=-1)
        xc = jax.lax.conv_general_dilated(xin.transpose(0, 2, 1), conv_w, (1,), [(D_CONV - 1, 0)], feature_group_count=D_INNER)
        xc = jax.nn.silu(xc + conv_b[None, :, None]).transpose(0, 2, 1)
        xdbl = xc @ x_proj_w.T
        dt = xdbl[..., :DT_RANK]
        Bm = xdbl[..., DT_RANK:DT_RANK + D_STATE]
        Cm = xdbl[..., DT_RANK + D_STATE:]
        dt = jax.nn.softplus(dt @ dt_proj_w.T + dt_proj_b)
        A = -jnp.exp(A_log)

        def step(h, inp):
            dt_t, B_t, C_t, x_t = inp
            dA = jnp.exp(dt_t[..., None] * A)
            h = dA * h + (dt_t * x_t)[..., None] * B_t[:, None, :]
            y = jnp.einsum('bdn,bn->bd', h, C_t)
            return (h, y)
        scan_xs = (dt.transpose(1, 0, 2), Bm.transpose(1, 0, 2), Cm.transpose(1, 0, 2), xc.transpose(1, 0, 2))
        h0 = jnp.zeros((B, D_INNER, D_STATE), xc.dtype)
        _, ys = jax.lax.scan(step, h0, scan_xs)
        y = ys.transpose(1, 0, 2) + xc * D
        y = y * jax.nn.silu(z)
        out = y @ out_proj_w.T
        out = _clamp(out)
        out = _layernorm(out, jnp.ones((C,), out.dtype), jnp.zeros((C,), out.dtype))
        out = out.transpose(0, 2, 1).reshape(B, C, H, W)
        return _clamp(out)

    def _L1_conv_ref(x, qkv_w, dw_w, pw_w, proj_w, bn_gamma, bn_beta, bn_mean, bn_var):
        import jax, jax.numpy as jnp
        import numpy as np
        DIM = 8
        HEADS = 32
        TOTAL = HEADS * DIM
        QKV_C = 3 * TOTAL
        PW_GROUPS = 3 * HEADS
        GSZ = QKV_C // PW_GROUPS
        EPS_ATT = 1e-15
        EPS_BN = 1e-05

        def _forward(x, qkv_w, dw_w, pw_w, proj_w, bn_gamma, bn_beta, bn_mean, bn_var):
            B, _, H, W = x.shape
            qkv = jnp.einsum('bchw,oc->bohw', x, qkv_w)
            agg = jax.lax.conv_general_dilated(qkv, dw_w, window_strides=(1, 1), padding=((2, 2), (2, 2)), feature_group_count=QKV_C, dimension_numbers=('NCHW', 'OIHW', 'NCHW'))
            agg = agg.reshape(B, PW_GROUPS, GSZ, H, W)
            agg = jnp.einsum('bgihw,goi->bgohw', agg, pw_w).reshape(B, QKV_C, H, W)
            qkv_cat = jnp.concatenate([qkv, agg], axis=1)
            N = H * W
            t = qkv_cat.reshape(B, -1, 3 * DIM, N)
            q = jax.nn.relu(t[:, :, :DIM])
            k = jax.nn.relu(t[:, :, DIM:2 * DIM])
            v = t[:, :, 2 * DIM:]
            v = jnp.concatenate([v, jnp.ones_like(v[:, :, :1])], axis=2)
            vk = jnp.einsum('bhdn,bhen->bhde', v, k)
            out = jnp.einsum('bhde,bhen->bhdn', vk, q)
            out = out[:, :, :-1] / (out[:, :, -1:] + EPS_ATT)
            out = out.reshape(B, -1, H, W)
            out = jnp.einsum('bchw,oc->bohw', out, proj_w)
            inv = bn_gamma / jnp.sqrt(bn_var + EPS_BN)
            out = out * inv[None, :, None, None] + (bn_beta - bn_mean * inv)[None, :, None, None]
            return out
        return _forward(x, qkv_w, dw_w, pw_w, proj_w, bn_gamma, bn_beta, bn_mean, bn_var)

    def _gn(v, G=32, eps=1e-05):
        B_, C_, H_, W_ = v.shape
        g = v.reshape(B_, G, C_ // G, H_, W_)
        m = jnp.mean(g, axis=(2, 3, 4), keepdims=True)
        s = jnp.var(g, axis=(2, 3, 4), keepdims=True)
        return ((g - m) / jnp.sqrt(s + eps)).reshape(v.shape)

    def _ln_c(v, eps=1e-06):
        m = jnp.mean(v, axis=1, keepdims=True)
        s = jnp.var(v, axis=1, keepdims=True)
        return (v - m) / jnp.sqrt(s + eps)

    def _ln_t(v, eps=1e-05):
        m = jnp.mean(v, axis=-1, keepdims=True)
        s = jnp.var(v, axis=-1, keepdims=True)
        return (v - m) / jnp.sqrt(s + eps)

    def _to_tokens(v):
        B_, C_, H_, W_ = v.shape
        return v.reshape(B_, C_, H_ * W_).transpose(0, 2, 1)

    def _from_tokens(t, like):
        B_, C_, H_, W_ = like.shape
        return t.transpose(0, 2, 1).reshape(B_, C_, H_, W_)
    x = x + _L0_conv_ref(_gn(x), L0_conv_norm_w, L0_conv_norm_b, L0_conv_in_proj_w, L0_conv_conv_w, L0_conv_conv_b, L0_conv_x_proj_w, L0_conv_dt_proj_w, L0_conv_dt_proj_b, L0_conv_A_log, L0_conv_D, L0_conv_out_proj_w)
    x = x + _L1_conv_ref(_gn(x), L1_conv_qkv_w, L1_conv_dw_w, L1_conv_pw_w, L1_conv_proj_w, L1_conv_bn_gamma, L1_conv_bn_beta, L1_conv_bn_mean, L1_conv_bn_var)
    return x

_drawn_inputs = setup_inputs


def setup_inputs(seed=0):
    import zlib

    import numpy as np

    out = dict(_drawn_inputs(seed))
    spreads = {'L0_conv_norm_w': (1.0, 0.2),
     'L0_conv_norm_b': (0.0, 0.1),
     'L0_conv_conv_b': (0.0, 0.1),
     'L0_conv_dt_proj_b': (-4.600166320800781, 0.6),
     'L0_conv_D': (1.0, 0.6),
     'L1_conv_bn_gamma': (1.0, 0.6),
     'L1_conv_bn_beta': (0.0, 0.1)}
    factors = {'L0_conv_x_proj_w': 28.817,
     'L0_conv_dt_proj_w': 60.778,
     'L0_conv_A_log': 31.373,
     'L1_conv_qkv_w': 5.535,
     'L1_conv_dw_w': 8.0,
     'L1_conv_pw_w': 8.0,
     'L1_conv_proj_w': 5.714,
     'L1_conv_bn_mean': 6.613,
     'L1_conv_bn_var': 8.0}
    for name, (base, spread) in spreads.items():
        noise = np.random.default_rng([zlib.crc32(name.encode()), seed]).standard_normal(out[name].shape)
        drawn = base * np.exp(spread * noise) if base else spread * noise
        out[name] = jnp.asarray(drawn.astype(out[name].dtype))
    for name, factor in factors.items():
        out[name] = (out[name] * factor).astype(out[name].dtype)
    return out
```

```python
from contextlib import ExitStack

import concourse.bass as bass
from concourse import mybir

ALU = mybir.AluOpType
ACT = mybir.ActivationFunctionType
F32 = mybir.dt.float32
BF16 = mybir.dt.bfloat16

P = 128
B = 2
C = 256
CT = C // P
HW = 32
L = HW * HW
HALF = 512
DI = 512
DT_ = DI // P
NS = 16
R = 16
XD = R + 2 * NS
KC = 4
OCT = P // NS
GT = P // OCT
NG = B * DT_
PARTS = 3
QC = 3 * C
QT = QC // P
HD = 8
PAD = 2
PW = HW + 2 * PAD
TAPS = 25
PE_TAPS = 10
DV_TAPS = TAPS - PE_TAPS
BLK = L // P
CAP = 2.0
LOG_A_CAP = 20.0
CLAMP = 10.0
EPS = 1e-5
EPS_ATT = 1e-15


def mamba_attention_kernel(nc, a, out):
    with ExitStack() as ctx:
        def sb(name, shape, dt=F32):
            return ctx.enter_context(nc.sbuf_tensor(name, shape, dt))

        def sem(name):
            return ctx.enter_context(nc.semaphore(name))

        X = sb("X", [P, B, CT, L])[:, :, :, :]
        arena = sb("arena", [P, 20480])
        mid = sb("mid", [P, 20480])

        def view(t, at, *shape):
            n = 1
            for s in shape:
                n *= s
            names = "abcd"[:len(shape)]
            pat = f"p ({' '.join(names)}) -> p {' '.join(names)}"
            return t[:, at:at + n].rearrange(pat, **dict(zip(names, shape)))

        XG = view(arena, 0, B, CT, L)
        SQ = view(arena, 4096, B, CT, L)
        RS = view(arena, 8192, B, L)
        XIN = view(arena, 10240, 2, L + KC)
        CA = view(arena, 12296, 2, L)
        XDB = view(arena, 17408, B, L)
        DTF = view(arena, 0, 3, L)
        VV = view(arena, 3072, 2, L)
        UM1 = arena[:, 19456:20480]
        DXF = view(arena, 5120, 2, L)
        dt_parts = arena[:, 7168:13312].bitcast(BF16).rearrange("p (r i l) -> p r i l", r=3, i=PARTS + 1)
        dx_parts = arena[:, 13312:16384].bitcast(BF16).rearrange("p (r i l) -> p r i l", r=2, i=PARTS)
        HT = arena[:, 16384:17408].bitcast(BF16).rearrange("p (r l) -> p r l", r=2)
        H = view(arena, 0, 4, L)
        G = view(arena, 4096, 8, L)
        stack = arena[:, 12288:20480].bitcast(BF16).rearrange("p (s k q l) -> p s k q l", s=2, k=2, q=4)
        XC = view(mid, 0, NG, L)
        SZ = view(mid, 8192, NG, L)
        BR = view(mid, 16384, B, L)
        CR = view(mid, 18432, B, L)
        PADB = arena[:, 0:B * QT * PW * PW].rearrange("p (b t y x) -> p b t y x", b=B, t=QT, y=PW)
        WT = view(arena, 15552, 2, PE_TAPS, P)
        ACC = view(arena, 18112, 2, HW, HW)
        XG2 = view(mid, 0, B, CT, L)
        QR = view(mid, 4096, 4, L)
        KT = view(mid, 8192, BLK, 4, P)
        VT = view(mid, 12288, BLK, 4, P + 1)
        TMP = view(mid, 16416, 2, L)

        WIN = sb("WIN", [P, CT, 2 * DI])
        LNB = WIN[:, :, :]
        WQ = WIN[:, :, 0:QC]
        WOUT = sb("WOUT", [P, DT_, C])
        WPR = sb("WPR", [P, 4, C])
        XPW = sb("XPW", [P, DT_, XD])
        DTW = sb("DTW", [P, DI])
        cst = sb("cst", [P, 6, P])
        GRP8, ONES, IDENT, REPB, REPC, MASK = (cst[:, i, :] for i in range(6))
        SELR = sb("SELR", [P, 4, 32])
        SELB = sb("SELB", [P, 4, P], BF16)
        SELX = X.rearrange("p b t l -> p (b t l)").bitcast(BF16).rearrange("p (g q j n) -> p g q j n", g=DT_, q=4, j=4)
        ALR = SZ[96:P].rearrange("p e l -> p (e l)").rearrange("p (o j n) -> p o j n", o=DT_ * 4, j=4)
        AC = sb("AC", [P, DI // OCT])
        COLS = sb("COLS", [P, 40])
        NW, NB = COLS[:, 0:2], COLS[:, 2:4]
        CW = COLS[:, 4:20].rearrange("p (t k) -> p t k", k=KC)
        CB, DTB, DD = COLS[:, 20:24], COLS[:, 24:28], COLS[:, 28:32]
        BNG, BNB, BNM, BNV = (COLS[:, 32 + 2 * i:34 + 2 * i] for i in range(4))
        DW = sb("DW", [P, QT, TAPS])
        PWN = sb("PWN", [P, QT, HD])
        PWB = sb("PWB", [P, QT, P])
        ST = sb("ST", [P, 4, 2, 6])
        MV = sb("MV", [P, 4, 2])
        GM = sb("GM", [P, 4])
        GV = sb("GV", [P, 4])
        GR = sb("GR", [P, 4])
        EPSC = sb("EPSC", [P, 1])
        INV = sb("INV", [P, 2])
        SHF = sb("SHF", [P, 2])
        KS = sb("KS", [P, 2])
        VKS = sb("VKS", [P, 2, 2, P])
        PS = ctx.enter_context(nc.psum_tensor("PS", [P, 8, HALF], F32))

        def pair(k):
            return PS[:, 2 * k:2 * k + 2, :].rearrange("p a b -> p (a b)")

        def bank(k, c):
            return PS[:, 2 * k + c, :]

        dt_scratch = nc.dram_tensor("dt_parts", (NG, PARTS + 1, P, L), BF16, kind="Internal").ap()
        dx_scratch = nc.dram_tensor("dx_parts", (NG, PARTS, P, L), BF16, kind="Internal").ap()

        names = """ld_x ld_c ld_w0 ld_w1 eps_set pad_set
            gn_stat gn_self gn_mu_ps gn_dev gn_v gn_var_ps gn_ln gn_rstd gn_out
            ln_mu_ps ln_cent ln_sq ln_var_ps ln_lnv ln_rstd ln_self ln_out
            ip_ps xin_rd conv_self conv_out xc_rd sz_rd
            xd_zero xd_ps xd_rd rep_ps brep_rd crep_rd
            dt_ps sp_abs sp_exp sp_ln um1_rd sp_corr sp_sum v_rd dt_rd dx_rd hi_rd dt_r dx_r mid_rd dt_lo dx_lo
            dt_st0 dt_st1 dt_st2 dx_st0 dx_st1 ld_sel ld_alr ld_x1 selx_rd ex_lim ex_rd hic_rd stk_zero stk_ld0 stk_ld1 a_exp a_rd
            bc_dt bc_dx da_rd u_rd scan_rd g_rd red_ps y_add y_rd
            op_ps op_rd x1_rd
            pwb_rd pad_zero bn_ln bn_self bn_rd qkv_ps pad_rd q_rd tr_ps kv_rd one_set
            wt_rd acc_self acc_rd cv_ps cv_rd tmp_rd vk_ps ks_rd vks_rd nd_ps den_self o_rd pr_ps pr_rd st_out""".split()
        S = {n: sem(n) for n in names}
        dt_st = [S[f"dt_st{r}"] for r in range(3)]
        dx_st = [S[f"dx_st{r}"] for r in range(2)]
        stk_ld = [S["stk_ld0"], S["stk_ld1"]]
        TILE_PS = 1

        block = ctx.enter_context(nc.Block())
        n_w0 = 0

        @block.sync
        def _(sp):
            for b in range(B):
                sp.dma_start(X[:, b], a["x"][b].rearrange("(t p) l -> p t l", p=P)).then_inc(S["ld_x"], 16)
            sp.dma_start(ALR, a["alogr"].rearrange("(z c) n -> z (c n)", z=1).broadcast_to([32, DI * NS])
                         .rearrange("p (o j n) -> p o j n", o=DT_ * 4, j=4)).then_inc(S["ld_alr"], 16)
            sp.dma_start(WIN[:, :, :], a["win"].rearrange("(t p) n -> p t n", p=P)).then_inc(S["ld_w0"], 16)
            sp.dma_start(XPW[:, :, :], a["xpw"].rearrange("(t p) n -> p t n", p=P)).then_inc(S["ld_w0"], 16)
            sp.wait_ge(S["pad_set"], 2)
            sp.dma_start(DTW[0:R, :], a["dtw"]).then_inc(S["ld_w0"], 16)
            sp.dma_start(AC[:, :], a["alog"]).then_inc(S["ld_w0"], 16)
            sp.dma_start(WOUT[:, :, :], a["wout"].rearrange("(t p) n -> p t n", p=P)).then_inc(S["ld_w0"], 16)
            sp.dma_start(WPR[:, :, :], a["wpr"].rearrange("(t p) n -> p t n", p=P)).then_inc(S["ld_w0"], 16)
            sp.dma_start(DW[:, :, :], a["dw"].rearrange("(t p) n -> p t n", p=P)).then_inc(S["ld_w0"], 16)
            sp.dma_start(PWN[:, :, :], a["pw"].rearrange("(t p) n -> p t n", p=P)).then_inc(S["ld_w0"], 16)
            sp.wait_ge(S["gn_out"], 4)
            for o in range(DT_ * 4):
                sp.dma_start(SELX[0:96, o // 4, o % 4], a["selb"][0:96]).then_inc(S["ld_sel"], 16)
            for e in range(NG):
                sp.wait_ge(S["dt_lo"], e + 1)
                sp.wait_ge(S["hic_rd"], e + 1)
                sp.dma_start(dt_scratch[e].rearrange("i p l -> p i l"), dt_parts[:, e % 3]).then_inc(dt_st[e % 3], 16)
                sp.wait_ge(S["dx_lo"], e + 1)
                sp.dma_start(dx_scratch[e].rearrange("i p l -> p i l"), dx_parts[:, e % 2]).then_inc(dx_st[e % 2], 16)
            for r in range(3):
                sp.wait_ge(dt_st[r], 16 * len(range(r, NG, 3)))
            for r in range(2):
                sp.wait_ge(dx_st[r], 16 * len(range(r, NG, 2)))
            sp.wait_ge(S["stk_zero"], 1)

            def load_stack(e, s, n):
                for k, scratch in enumerate((dt_scratch, dx_scratch)):
                    for i in range(PARTS + 1 - k):
                        sp.dma_start(stack[32 * i:32 * i + 32, s, k],
                                     scratch[e, i].rearrange("(q c) l -> c q l", c=32)).then_inc(stk_ld[s], 16)

            load_stack(0, 0, 0)
            load_stack(1, 1, 0)
            with sp.Fori(1, NG // 2) as n:
                for s in range(2):
                    sp.wait_ge(S["bc_dt"], 16 * (2 * n + s) - 16)
                    load_stack(2 * n + s, s, n)
            sp.wait_ge(S["dt_rd"], NG)
            sp.dma_start(WQ, a["wq"].rearrange("(t p) n -> p t n", p=P)).then_inc(S["ld_w1"], 16)
            sp.wait_ge(S["bc_dt"], GT * NG)
            for b in range(B):
                sp.dma_start(X[:, b], a["x"][b].rearrange("(t p) l -> p t l", p=P)).then_inc(S["ld_x1"], 16)
            for b in range(B):
                for m in range(CT):
                    sp.wait_ge(S["pr_rd"], CT * b + m + 1)
                    sp.dma_start(out[b, m * P:(m + 1) * P, :], X[:, b, m]).then_inc(S["st_out"], 16)
            sp.wait_ge(S["st_out"], 16 * B * CT)

        @block.gpsimd
        def _(pool):
            pool.memset(EPSC[:, :], EPS).then_inc(S["eps_set"], 1)
            pool.memset(XIN[:, :, 0:KC - 1], 0.0).then_inc(S["pad_set"], 1)
            pool.memset(DTW[:, :], 0.0).then_inc(S["pad_set"], 1)
            pool.memset(XDB[:, :, :], 0.0).then_inc(S["xd_zero"], 1)
            pool.wait_ge(S["ld_w0"], 128)
            pool.wait_ge(S["ld_c"], 64)
            for t in range(QT):
                pool.tensor_tensor(PWB[:, t, :].rearrange("p (g o) -> p g o", o=HD),
                                   MASK.rearrange("p (g o) -> p g o", o=HD),
                                   PWN[:, t:t + 1, :].broadcast_to([P, P // HD, HD]), ALU.mult).then_inc(S["pwb_rd"], 1)
            for i in range(NG + 2):
                if i < NG:
                    pool.wait_ge(S["sp_ln"], i + 1)
                    pool.wait_ge(S["um1_rd"], i + 1)
                    pool.tensor_tensor(LNB[:, i % 2], LNB[:, i % 2], UM1[:, :], ALU.subtract).then_inc(S["sp_corr"], 1)
                if i >= 2:
                    e = i - 2
                    pool.wait_ge(S["mid_rd"], 2 * e + 2)
                    pool.tensor_tensor(dx_parts[:, e % 2, 2], DXF[:, e % 2], dx_parts[:, e % 2, 1], ALU.subtract).then_inc(S["dx_lo"], 1)
                if 1 <= i <= NG:
                    e = i - 1
                    pool.wait_ge(S["hi_rd"], 2 * e + 2)
                    pool.tensor_tensor(DXF[:, e % 2], DXF[:, e % 2], dx_parts[:, e % 2, 0], ALU.subtract).then_inc(S["dx_r"], 1)
            for r in range(3):
                pool.wait_ge(dt_st[r], 16 * len(range(r, NG, 3)))
            for r in range(2):
                pool.wait_ge(dx_st[r], 16 * len(range(r, NG, 2)))
            pool.wait_ge(S["dt_ps"], NG)
            pool.memset(stack[96:P, :, 1], 0.0).then_inc(S["stk_zero"], 1)

            def mult_c(it, b, first):
                for t in range(GT):
                    pool.wait_ge(S["scan_rd"], GT * it + t + 1)
                    if not first or t >= 8:
                        pool.wait_ge(S["red_ps"], 4 * it + t // 4 - 1)
                    pool.tensor_tensor(G[:, t % 8], H[:, t % 4], CR[:, b], ALU.mult).then_inc(S["g_rd"], 1)
                    if t == 9 and not first:
                        gate(it - 1)

            def gate(it):
                pool.wait_ge(S["y_add"], it + 1)
                pool.wait_ge(S["sz_rd"], NG)
                pool.tensor_tensor(XC[:, it], XC[:, it], SZ[:, it], ALU.mult).then_inc(S["y_rd"], 1)

            pool.wait_ge(S["crep_rd"], B)
            mult_c(0, 0, True)
            for b in range(B):
                with pool.Fori(max(1, b * DT_), (b + 1) * DT_) as it:
                    mult_c(it, b, False)
            gate(NG - 1)
            pool.wait_ge(S["x1_rd"], B * CT)
            images = PADB.rearrange("p b t y x -> p (b t) y x")
            for edge in (slice(0, PAD), slice(PAD + HW, PW)):
                pool.memset(images[:, :, edge, :], 0.0).then_inc(S["pad_zero"], 1)
                pool.memset(images[:, :, PAD:PAD + HW, edge], 0.0).then_inc(S["pad_zero"], 1)
            pool.wait_ge(S["op_ps"], B * CT)
            pool.memset(VT[:, :, :, P:P + 1], 1.0).then_inc(S["one_set"], 1)
            pool.wait_ge(S["red_ps"], 4 * NG)
            for n in range(B * QT):
                if n >= 2:
                    pool.wait_ge(S["cv_ps"], n - 1)
                t = n % QT
                pool.tensor_tensor(WT[:, n % 2], PWB[:, t:t + 1, :].broadcast_to([P, PE_TAPS, P]),
                                   DW[:, t, 0:PE_TAPS].unsqueeze(2).broadcast_to([P, PE_TAPS, P]), ALU.mult).then_inc(S["wt_rd"], 1)

        @block.scalar
        def _(act):
            act.dma_start(cst[:, :, :], a["cst"]).then_inc(S["ld_c"], 16)
            act.dma_start(SELR[:, :, :], a["selr"]).then_inc(S["ld_c"], 16)
            act.dma_start(SELB[:, :, :], a["selb"]).then_inc(S["ld_c"], 16)
            act.dma_start(COLS[:, :], a["cols"]).then_inc(S["ld_c"], 16)
            act.wait_ge(S["eps_set"], 1)

            def group_rstd(ph):
                act.wait_ge(S["gn_var_ps"], ph + 1)
                act.activation(GR[:, :], PS[:, 1, 0:4], ACT.Ln, bias=EPSC[:, :]).then_inc(S["gn_ln"], 1)
                act.wait_ge(S["gn_ln"], ph + 1)
                act.activation(GR[:, :], GR[:, :], ACT.Exp, scale=-0.5).then_inc(S["gn_rstd"], 1)

            def pixel_rstd(ph):
                for b in range(B):
                    n = B * ph + b
                    for t in range(CT):
                        act.wait_ge(S["ln_cent"], CT * n + t + 1)
                        act.activation(SQ[:, b, t], XG[:, b, t], ACT.Square).then_inc(S["ln_sq"], 1)
                    act.wait_ge(S["ln_var_ps"], n + 1)
                    act.activation(RS[:, b], pair(2 + b), ACT.Ln, bias=EPSC[:, :]).then_inc(S["ln_lnv"], 1)
                    act.wait_ge(S["ln_lnv"], n + 1)
                    act.activation(RS[:, b], RS[:, b], ACT.Exp, scale=-0.5).then_inc(S["ln_rstd"], 1)

            group_rstd(0)
            act.wait_ge(S["ld_w0"], 128)
            act.activation(AC[:, :], AC[:, :], ACT.Exp).then_inc(S["a_exp"], 1)
            pixel_rstd(0)

            def silu_xc(e):
                act.wait_ge(S["conv_out"], e + 1)
                act.activation(XC[:, e], CA[:, e % 2], ACT.Silu, bias=CB[:, e % DT_:e % DT_ + 1]).then_inc(S["xc_rd"], 1)

            act.wait_ge(S["pad_set"], 2)
            act.wait_ge(S["selx_rd"], 4)
            for b in range(B):
                for m in range(2 * DT_):
                    k = 2 * DT_ * b + m
                    act.wait_ge(S["ip_ps"], k + 1)
                    if m < DT_:
                        e = DT_ * b + m
                        if e >= 2:
                            act.wait_ge(S["conv_out"], e - 1)
                            act.wait_ge(S["xc_rd"], e - 1)
                        act.activation(XIN[:, e % 2, KC - 1:KC - 1 + L], pair(k % 4), ACT.Copy).then_inc(S["xin_rd"], 1)
                        act.activation(CA[:, e % 2], pair(k % 4), ACT.Copy, scale=CW[:, m, KC - 1:KC]).then_inc(S["xin_rd"], 1)
                    else:
                        act.activation(SZ[:, DT_ * b + m - DT_], pair(k % 4), ACT.Silu).then_inc(S["sz_rd"], 1)
                    if 1 <= m <= DT_:
                        silu_xc(DT_ * b + m - 1)
            for b in range(B):
                act.wait_ge(S["xd_ps"], b + 1)
                act.wait_ge(S["xd_zero"], 1)
                act.activation(XDB[0:XD, b], pair(b)[0:XD, :], ACT.Copy).then_inc(S["xd_rd"], 1)
            for b in range(B):
                act.wait_ge(S["rep_ps"], 2 * b + 2)
                act.activation(CR[:, b], pair(2 * b + 1), ACT.Copy).then_inc(S["crep_rd"], 1)

            for i in range(NG + 2):
                if i < NG:
                    if i >= 3:
                        act.wait_ge(S["dt_lo"], i - 2)
                    act.wait_ge(S["v_rd"], i + 1)
                    act.activation(DTF[:, i % 3], VV[:, i % 2], ACT.Abs).then_inc(S["sp_abs"], 1)
                    act.wait_ge(S["sp_abs"], i + 1)
                    act.activation(DTF[:, i % 3], DTF[:, i % 3], ACT.Exp, scale=-1.0).then_inc(S["sp_exp"], 1)
                    if i >= 2:
                        act.wait_ge(S["dt_rd"], i - 1)
                    act.wait_ge(S["sp_exp"], i + 1)
                    act.activation(LNB[:, i % 2], DTF[:, i % 3], ACT.Ln, bias=1.0).then_inc(S["sp_ln"], 1)
                if i >= 2:
                    e = i - 2
                    act.wait_ge(S["dt_r"], e + 1)
                    act.activation(dt_parts[:, e % 3, 1], DTF[:, e % 3], ACT.Copy).then_inc(S["mid_rd"], 1)
                    act.wait_ge(S["dx_r"], e + 1)
                    act.activation(dx_parts[:, e % 2, 1], DXF[:, e % 2], ACT.Copy).then_inc(S["mid_rd"], 1)
                if 1 <= i <= NG:
                    e = i - 1
                    if e >= 3:
                        act.wait_ge(dt_st[e % 3], 16 * (e // 3))
                    if e >= 2:
                        act.wait_ge(dx_st[e % 2], 16 * (e // 2))
                        act.wait_ge(S["hic_rd"], e - 1)
                    act.wait_ge(S["dt_rd"], e + 1)
                    act.activation(HT[:, e % 2], DTF[:, e % 3], ACT.Copy).then_inc(S["hi_rd"], 1)
                    act.wait_ge(S["dx_rd"], e + 1)
                    act.activation(dx_parts[:, e % 2, 0], DXF[:, e % 2], ACT.Copy).then_inc(S["hi_rd"], 1)
            act.wait_ge(S["a_rd"], 1)
            with act.Fori(0, NG) as it:
                g = it & (DT_ - 1)
                for t in range(GT):
                    act.wait_ge(S["bc_dt"], GT * it + t + 1)
                    octave = GT * g + 4 * (t % 4) + t // 4
                    act.activation(pair(t % 2), pair(t % 2), ACT.Exp, scale=AC[:, bass.ds(octave, 1)]).then_inc(S["da_rd"], 1)
            pixel_rstd(1)
            group_rstd(1)
            act.activation(INV[:, :], BNV, ACT.Ln, bias=EPSC[:, :]).then_inc(S["bn_ln"], 1)
            act.wait_ge(S["bn_ln"], 1)
            act.activation(INV[:, :], INV[:, :], ACT.Exp, scale=-0.5).then_inc(S["bn_ln"], 1)

            def copy_kv(n, k):
                if n % 8 == 0 and n:
                    act.wait_ge(S["o_rd"], n // 2)
                if n >= 2:
                    act.wait_ge(S["tr_ps"], n - 1)
                act.activation(TMP[:, n % 2], pair(k), ACT.Copy).then_inc(S["tmp_rd"], 1)

            def evac_kv(n):
                b, w = divmod(n, 8)
                act.wait_ge(S["tr_ps"], n + 1)
                path, i = divmod(w, 4)
                src = pair(3).rearrange("p (k c) -> p k c", c=P)
                if w == 0 and b:
                    act.wait_ge(S["vk_ps"], 4 * b)
                if i < 2:
                    act.activation(KT[:, :, 2 * path + i, :], src, ACT.Relu).then_inc(S["kv_rd"], 1)
                else:
                    act.activation(VT[:, :, 2 * path + i - 2, 0:P], src, ACT.Copy).then_inc(S["kv_rd"], 1)

            act.wait_ge(S["one_set"], 1)
            act.wait_ge(S["pad_zero"], 4)
            for b in range(B):
                for t in range(QT):
                    k = QT * b + t
                    act.wait_ge(S["qkv_ps"], k + 1)
                    act.activation(PADB[:, b, t, PAD:PAD + HW, PAD:PAD + HW],
                                   pair(k % 3).rearrange("p (y x) -> p y x", x=HW), ACT.Copy).then_inc(S["pad_rd"], 1)
                    if t >= 2:
                        copy_kv(8 * b + t - 2, k % 3)
                    if t >= 3:
                        evac_kv(8 * b + t - 3)
                evac_kv(8 * b + 3)
                for t in range(QT):
                    n = QT * b + t
                    act.wait_ge(S["cv_ps"], n + 1)
                    if t < 2:
                        act.activation(QR[:, 2 + t], pair(n % 2), ACT.Relu).then_inc(S["cv_rd"], 1)
                    else:
                        copy_kv(8 * b + 4 + t - 2, n % 2)
                        evac_kv(8 * b + 4 + t - 2)

        @block.tensor
        def _(pe):
            pe.wait_ge(S["ld_c"], 64)

            def group_stats(ph):
                pe.wait_ge(S["gn_stat"], 4 * (ph + 1))
                pe.matmul(PS[:, 0, 0:4], GRP8, MV[:, :, 0], start=True, stop=True).then_inc(S["gn_mu_ps"], 1)
                pe.wait_ge(S["gn_v"], ph + 1)
                pe.matmul(PS[:, 1, 0:4], GRP8, GV[:, :], start=True, stop=True).then_inc(S["gn_var_ps"], 1)

            def pixel_stats(ph, ready, count):
                for b in range(B):
                    pe.wait_ge(ready, count * (b + 1))
                    for c in range(2):
                        for t in range(CT):
                            mm = pe.matmul(bank(b, c), ONES, XG[:, b, t, c * HALF:(c + 1) * HALF], start=(t == 0), stop=(t == CT - 1))
                    mm.then_inc(S["ln_mu_ps"], 1)
                for b in range(B):
                    pe.wait_ge(S["ln_sq"], CT * (B * ph + b + 1))
                    for c in range(2):
                        for t in range(CT):
                            mm = pe.matmul(bank(2 + b, c), ONES, SQ[:, b, t, c * HALF:(c + 1) * HALF], start=(t == 0), stop=(t == CT - 1))
                    mm.then_inc(S["ln_var_ps"], 1)

            group_stats(0)
            pe.wait_ge(S["gn_rstd"], 1)
            pe.wait_ge(S["gn_dev"], 1)
            pixel_stats(0, S["gn_out"], CT)
            pe.wait_ge(S["ln_rstd"], B)
            pe.wait_ge(S["ln_cent"], B * CT)
            pe.wait_ge(S["ld_w0"], 128)
            evac0 = []
            for b in range(B):
                pe.wait_ge(S["ln_out"], CT * (b + 1))
                for m in range(2 * DT_):
                    k = 2 * DT_ * b + m
                    if k >= 4:
                        kb, km = divmod(k - 4, 2 * DT_)
                        if km < DT_:
                            pe.wait_ge(S["xin_rd"], 2 * (DT_ * kb + km + 1))
                        else:
                            pe.wait_ge(S["sz_rd"], DT_ * kb + km - DT_ + 1)
                    for c in range(2):
                        for t in range(CT):
                            mm = pe.matmul(bank(k % 4, c), WIN[:, t, m * P:(m + 1) * P], XG[:, b, t, c * HALF:(c + 1) * HALF], start=(t == 0), stop=(t == CT - 1))
                    mm.then_inc(S["ip_ps"], 1)
            pe.wait_ge(S["sz_rd"], NG)
            for b in range(B):
                pe.wait_ge(S["xc_rd"], DT_ * (b + 1))
                for c in range(2):
                    for t in range(DT_):
                        mm = pe.matmul(bank(b, c)[0:XD, :], XPW[:, t, :], XC[:, DT_ * b + t, c * HALF:(c + 1) * HALF], start=(t == 0), stop=(t == DT_ - 1))
                mm.then_inc(S["xd_ps"], 1)
            for b in range(B):
                pe.wait_ge(S["xd_rd"], B)
                for i, rep in enumerate((REPB, REPC)):
                    for c in range(2):
                        mm = pe.matmul(bank(2 * b + i, c), rep, XDB[:, b, c * HALF:(c + 1) * HALF], start=True, stop=True)
                    mm.then_inc(S["rep_ps"], 1)
            pe.wait_ge(S["pad_set"], 2)
            for e in range(NG):
                if e < 4:
                    pe.wait_ge(S["brep_rd"] if e % 2 == 0 else S["crep_rd"], e // 2 + 1)
                else:
                    pe.wait_ge(S["v_rd"], e - 3)
                for c in range(2):
                    mm = pe.matmul(bank(e % 4, c), DTW[:, (e % DT_) * P:(e % DT_ + 1) * P], XDB[:, e // DT_, c * HALF:(c + 1) * HALF], start=True, stop=True)
                mm.then_inc(S["dt_ps"], 1)
            pe.wait_ge(S["v_rd"], NG)

            def spread(it, g, s, t, first):
                if t == 0:
                    pe.wait_ge(stk_ld[s], 112 * ((it >> 1) + 1))
                if not first or t >= 1:
                    pe.wait_ge(S["u_rd"], GT * it + t)
                for c in range(2):
                    mm = pe.matmul(bank(2, c), SELX[:, g, t % 4, t // 4, :], stack[:, s, 1, t % 4, c * HALF:(c + 1) * HALF], start=True, stop=True)
                mm.then_inc(S["bc_dx"], 1)
                if not first or t >= 2:
                    pe.wait_ge(S["scan_rd"], GT * it + t - 1)
                for c in range(2):
                    mm = pe.matmul(bank(t % 2, c), SELX[:, g, t % 4, t // 4, :], stack[:, s, 0, t % 4, c * HALF:(c + 1) * HALF], start=True, stop=True)
                mm.then_inc(S["bc_dt"], 1)

            def state_sum(it, k, c, first):
                if c == 0:
                    pe.wait_ge(S["g_rd"], GT * it + 4 * k + 4)
                if k == 0 and c == 0 and not first:
                    pe.wait_ge(S["y_add"], it)
                for q in range(4):
                    mm = pe.matmul(bank(3, c)[32 * q:32 * q + 32, :], SELR[:, k, :], G[:, (4 * k + q) % 8, c * HALF:(c + 1) * HALF],
                                   start=(k == 0), stop=(k == 3))
                if c:
                    mm.then_inc(S["red_ps"], 1)

            def group(it, s, first):
                g = 0 if first else it & (DT_ - 1)
                for t in range(GT):
                    spread(it, g, s, t, first)
                    if t in (2, 3):
                        if not first:
                            state_sum(it - 1, 3, t - 2, False)
                    elif t % 4 >= 2:
                        state_sum(it, t // 4 - 1, t % 4 - 2, first)

            pe.wait_ge(S["ld_sel"], 16 * DT_ * 4)
            pe.wait_ge(S["selx_rd"], 4)
            group(0, 0, True)
            with pe.Fori(0, NG // 2 - 1) as n:
                group(2 * n + 1, 1, False)
                group(2 * n + 2, 0, False)
            group(NG - 1, 1, False)
            for c in range(2):
                state_sum(NG - 1, 3, c, False)
            for b in range(B):
                pe.wait_ge(S["y_rd"], DT_ * (b + 1))
                for m in range(CT):
                    k = CT * b + m
                    if b == 0 and m == 0:
                        pe.wait_ge(S["scan_rd"], GT * NG)
                        pe.wait_ge(S["u_rd"], GT * NG)
                        pe.wait_ge(S["y_add"], NG)
                    for c in range(2):
                        for t in range(DT_):
                            mm = pe.matmul(bank(k, c), WOUT[:, t, m * P:(m + 1) * P], XC[:, DT_ * b + t, c * HALF:(c + 1) * HALF], start=(t == 0), stop=(t == DT_ - 1))
                    mm.then_inc(S["op_ps"], 1)
            pe.wait_ge(S["op_rd"], B * CT)
            pixel_stats(1, S["op_rd"], CT)
            pe.wait_ge(S["ln_rstd"], 2 * B)
            pe.wait_ge(S["ln_cent"], 2 * B * CT)
            group_stats(1)
            pe.wait_ge(S["gn_rstd"], 2)
            pe.wait_ge(S["ld_w1"], 16)

            def to_pixels(n):
                pe.wait_ge(S["tmp_rd"], n + 1)
                if n >= 1:
                    pe.wait_ge(S["kv_rd"], n)
                for j in range(BLK):
                    mm = pe.transpose(bank(3, j // 4)[:, (j % 4) * P:(j % 4 + 1) * P], TMP[:, n % 2, j * P:(j + 1) * P], IDENT)
                mm.then_inc(S["tr_ps"], 1)

            for b in range(B):
                pe.wait_ge(S["gn_out"], 4 + CT * (b + 1))
                if b:
                    pe.wait_ge(S["pr_rd"], CT * b)
                for t in range(QT):
                    k = QT * b + t
                    if t >= 3:
                        pe.wait_ge(S["pad_rd"], k - 2)
                        if t == 5:
                            pe.wait_ge(S["tmp_rd"], 8 * b + 1)
                    for c in range(2):
                        for u in range(CT):
                            mm = pe.matmul(bank(k % 3, c), WQ[:, u, t * P:(t + 1) * P], XG2[:, b, u, c * HALF:(c + 1) * HALF], start=(u == 0), stop=(u == CT - 1))
                    mm.then_inc(S["qkv_ps"], 1)
                for i in range(4):
                    to_pixels(8 * b + i)
                for t in range(QT):
                    n = QT * b + t
                    pe.wait_ge(S["wt_rd"], n + 1)
                    if t < 2:
                        pe.wait_ge(S["pad_rd"], QT * (b + 1))
                    elif t < 4:
                        pe.wait_ge(S["cv_rd"], 2 * b + t - 1)
                    else:
                        pe.wait_ge(S["tmp_rd"], 8 * b + 4 + t - 3)
                    for c in range(2):
                        for k in range(PE_TAPS):
                            dy, dx = divmod(k, 5)
                            pe.matmul(bank(n % 2, c), WT[:, n % 2, k, :],
                                      PADB[:, b, t, dy + 16 * c:dy + 16 * c + 16, dx:dx + HW], start=(k == 0), stop=False)
                        pe.wait_ge(S["acc_rd"], n + 1)
                        mm = pe.matmul(bank(n % 2, c), PWB[:, t, :], ACC[:, n % 2, 16 * c:16 * c + 16, :], start=False, stop=True)
                    mm.then_inc(S["cv_ps"], 1)
                    if t >= 3:
                        to_pixels(8 * b + 4 + t - 3)
                to_pixels(8 * b + 7)
                for w in range(4):
                    n = 4 * b + w
                    if w == 0:
                        pe.wait_ge(S["kv_rd"], 8 * (b + 1))
                    for j in range(BLK):
                        mm = pe.matmul(PS[:, 6, 0:P + 1], KT[:, j, w, :], VT[:, j, w, :], start=(j == 0), stop=(j == BLK - 1))
                    mm.then_inc(S["vk_ps"], 1)
                    pe.wait_ge(S["vks_rd"], 2 * n + 2)
                    if w == 0:
                        pe.wait_ge(S["q_rd"], 2 * (b + 1))
                        pe.wait_ge(S["cv_rd"], 2 * (b + 1))
                        pe.wait_ge(S["tmp_rd"], 8 * (b + 1))
                    if n >= 1:
                        pe.wait_ge(S["o_rd"], n)
                    for i in range(2):
                        for c in range(2):
                            mm = pe.matmul(bank(i, c), VKS[:, n % 2, i, :], QR[:, w, c * HALF:(c + 1) * HALF], start=True, stop=True)
                        mm.then_inc(S["nd_ps"], 1)
                pe.wait_ge(S["o_rd"], 4 * (b + 1))
                for m in range(CT):
                    for c in range(2):
                        for w in range(4):
                            mm = pe.matmul(bank(m, c), WPR[:, w, m * P:(m + 1) * P], QR[:, w, c * HALF:(c + 1) * HALF], start=(w == 0), stop=(w == 3))
                    mm.then_inc(S["pr_ps"], 1)

        @block.vector
        def _(dve):
            def group_norm(ph, dst):
                for i in range(4):
                    b, t = divmod(i, CT)
                    if ph == 0:
                        if t == 0:
                            dve.wait_ge(S["ld_x"], 32)
                    for c in range(2):
                        dve.bn_stats(ST[:, i, c, :], X[:, b, t, c * HALF:(c + 1) * HALF]).then_inc(S["gn_self"], 1)
                    dve.wait_ge(S["gn_self"], 14 * ph + 2 * i + 2)
                    dve.bn_aggr(MV[:, i, :], ST[:, i, :, :]).then_inc(S["gn_stat"], 1)
                dve.wait_ge(S["gn_mu_ps"], ph + 1)
                dve.tensor_copy(GM[:, :], PS[:, 0, 0:4]).then_inc(S["gn_self"], 1)
                dve.wait_ge(S["gn_self"], 14 * ph + 9)
                dve.tensor_tensor(GV[:, :], MV[:, :, 0], GM[:, :], ALU.subtract).then_inc(S["gn_dev"], 1)
                dve.wait_ge(S["gn_dev"], ph + 1)
                dve.tensor_tensor(GV[:, :], GV[:, :], GV[:, :], ALU.mult).then_inc(S["gn_self"], 1)
                dve.wait_ge(S["gn_self"], 14 * ph + 10)
                dve.tensor_tensor(GV[:, :], GV[:, :], MV[:, :, 1], ALU.add).then_inc(S["gn_v"], 1)
                dve.wait_ge(S["gn_rstd"], ph + 1)
                for i in range(4):
                    b, t = divmod(i, CT)
                    ins = dve.tensor_scalar(dst[:, b, t], X[:, b, t], GM[:, i:i + 1], GR[:, i:i + 1], ALU.subtract, ALU.mult)
                    if ph == 0:
                        ins.then_inc(S["gn_self"], 1)
                        dve.wait_ge(S["gn_self"], 11 + i)
                        ins = dve.tensor_scalar(dst[:, b, t], dst[:, b, t], CLAMP, -CLAMP, ALU.min, ALU.max)
                    ins.then_inc(S["gn_out"], 1)

            def pixel_norm(ph):
                for b in range(B):
                    n = B * ph + b
                    dve.wait_ge(S["ln_mu_ps"], n + 1)
                    for t in range(CT):
                        dve.tensor_tensor(XG[:, b, t], XG[:, b, t], pair(b), ALU.subtract).then_inc(S["ln_cent"], 1)
                for b in range(B):
                    n = B * ph + b
                    dve.wait_ge(S["ln_rstd"], n + 1)
                    for t in range(CT):
                        i = 2 * CT * b + 2 * t + 8 * ph
                        if ph == 1:
                            i = 8 + 2 * CT * b + 2 * t
                        dve.wait_ge(S["ln_cent"], CT * n + t + 1)
                        dve.tensor_tensor(XG[:, b, t], XG[:, b, t], RS[:, b], ALU.mult).then_inc(S["ln_self"], 1)
                        dve.wait_ge(S["ln_self"], i + 1)
                        if ph == 0:
                            dve.tensor_scalar(XG[:, b, t], XG[:, b, t], NW[:, t:t + 1], NB[:, t:t + 1], ALU.mult, ALU.add).then_inc(S["ln_self"], 1)
                            dve.wait_ge(S["ln_self"], i + 2)
                            dve.tensor_scalar(XG[:, b, t], XG[:, b, t], CLAMP, -CLAMP, ALU.min, ALU.max).then_inc(S["ln_out"], 1)
                        else:
                            dve.tensor_scalar(XG[:, b, t], XG[:, b, t], CLAMP, -CLAMP, ALU.min, ALU.max).then_inc(S["ln_self"], 1)
                            dve.wait_ge(S["ln_self"], i + 2)
                            dve.wait_ge(S["ld_x1"], 32)
                            dve.tensor_tensor(X[:, b, t], X[:, b, t], XG[:, b, t], ALU.add).then_inc(S["x1_rd"], 1)

            dve.wait_ge(S["ld_c"], 64)
            group_norm(0, XG)
            dve.wait_ge(S["ld_alr"], 16)
            dve.wait_ge(S["gn_out"], 4)
            for j in range(4):
                dve.scalar_tensor_tensor(out=SELX[96:P].rearrange("p g q j n -> p (g q) j n")[:, :, j, :], in0=ALR[:, :, j, :], scalar=LOG_A_CAP,
                                         in1=SELB[96:P, j:j + 1, :].broadcast_to([32, DT_ * 4, P]), op0=ALU.is_le, op1=ALU.mult).then_inc(S["selx_rd"], 1)
            pixel_norm(0)
            dve.wait_ge(S["a_exp"], 1)
            dve.tensor_scalar(AC[:, :], AC[:, :], -1.0, None, ALU.mult).then_inc(S["a_rd"], 1)
            for e in range(NG):
                m = e % DT_
                dve.wait_ge(S["xin_rd"], 2 * e + 2)
                for k in range(KC - 1):
                    if k:
                        dve.wait_ge(S["conv_self"], 2 * e + k)
                    ins = dve.scalar_tensor_tensor(out=CA[:, e % 2], in0=XIN[:, e % 2, k:k + L], scalar=CW[:, m, k:k + 1], in1=CA[:, e % 2], op0=ALU.mult, op1=ALU.add)
                    ins.then_inc(S["conv_out"] if k == KC - 2 else S["conv_self"], 1)
            for b in range(B):
                dve.wait_ge(S["rep_ps"], 2 * b + 1)
                dve.tensor_copy(BR[:, b], pair(2 * b)).then_inc(S["brep_rd"], 1)

            for i in range(NG + 2):
                if i < NG:
                    dve.wait_ge(S["dt_ps"], i + 1)
                    if i >= 2:
                        dve.wait_ge(S["sp_abs"], i - 1)
                        dve.wait_ge(S["dt_rd"], i - 1)
                    dve.tensor_scalar(VV[:, i % 2], pair(i % 4), DTB[:, i % DT_:i % DT_ + 1], None, ALU.add).then_inc(S["v_rd"], 1)
                    if i >= 1:
                        dve.wait_ge(S["sp_corr"], i)
                    dve.wait_ge(S["sp_exp"], i + 1)
                    dve.tensor_scalar(UM1[:, :], DTF[:, i % 3], 1.0, 1.0, ALU.add, ALU.subtract).then_inc(S["um1_rd"], 1)
                if i >= 2:
                    e = i - 2
                    dve.wait_ge(S["mid_rd"], 2 * e + 1)
                    dve.tensor_tensor(dt_parts[:, e % 3, 2], DTF[:, e % 3], dt_parts[:, e % 3, 1], ALU.subtract).then_inc(S["dt_lo"], 1)
                if 1 <= i <= NG:
                    e = i - 1
                    dve.wait_ge(S["sp_corr"], e + 1)
                    dve.scalar_tensor_tensor(out=DTF[:, e % 3], in0=LNB[:, e % 2], scalar=0.0, in1=DTF[:, e % 3], op0=ALU.min, op1=ALU.add).then_inc(S["sp_sum"], 1)
                    dve.wait_ge(S["sp_sum"], e + 1)
                    dve.scalar_tensor_tensor(out=DTF[:, e % 3], in0=VV[:, e % 2], scalar=0.0, in1=DTF[:, e % 3], op0=ALU.max, op1=ALU.add).then_inc(S["dt_rd"], 1)
                    dve.wait_ge(S["dt_rd"], e + 1)
                    if e >= 2:
                        dve.wait_ge(S["dx_lo"], e - 1)
                    dve.tensor_tensor(DXF[:, e % 2], DTF[:, e % 3], XC[:, e], ALU.mult).then_inc(S["dx_rd"], 1)
                    dve.wait_ge(S["hi_rd"], 2 * e + 1)
                    dve.wait_ge(S["dx_rd"], e + 1)
                    dve.tensor_tensor(DTF[:, e % 3], DTF[:, e % 3], HT[:, e % 2], ALU.subtract).then_inc(S["dt_r"], 1)
                    if e >= 3:
                        dve.wait_ge(dt_st[e % 3], 16 * (e // 3))
                    dve.tensor_scalar(dt_parts[:, e % 3, 3], HT[:, e % 2], CAP, 0.0, ALU.subtract, ALU.max).then_inc(S["ex_lim"], 1)
                    dve.wait_ge(S["ex_lim"], e + 1)
                    dve.scalar_tensor_tensor(out=dt_parts[:, e % 3, 3], in0=HT[:, e % 2], scalar=63.0 / 64, in1=dt_parts[:, e % 3, 3],
                                             op0=ALU.mult, op1=ALU.min).then_inc(S["ex_rd"], 1)
                    dve.wait_ge(S["ex_rd"], e + 1)
                    dve.tensor_tensor(dt_parts[:, e % 3, 0], HT[:, e % 2], dt_parts[:, e % 3, 3], ALU.subtract).then_inc(S["hic_rd"], 1)

            def take_u(it, b, t, first):
                dve.wait_ge(S["bc_dx"], GT * it + t + 1)
                if not first or t >= 4:
                    dve.wait_ge(S["g_rd"], GT * it + t - 3)
                dve.tensor_tensor(H[:, t % 4], pair(2), BR[:, b], ALU.mult).then_inc(S["u_rd"], 1)

            def scan(it, t):
                dve.wait_ge(S["da_rd"], GT * it + t + 1)
                dve.wait_ge(S["u_rd"], GT * it + t + 1)
                dve.tensor_tensor_scan(H[:, t % 4], pair(t % 2), H[:, t % 4], 0.0, ALU.mult, ALU.add).then_inc(S["scan_rd"], 1)

            def add_skip(it, g):
                dve.wait_ge(S["red_ps"], 4 * it + 4)
                dve.scalar_tensor_tensor(out=XC[:, it], in0=XC[:, it], scalar=DD[:, bass.ds(g, 1)], in1=pair(3), op0=ALU.mult, op1=ALU.add).then_inc(S["y_add"], 1)

            def group(it, first):
                b = 0 if first else (it >> 2) & 1
                for t in range(GT):
                    take_u(it, b, t, first)
                    if t:
                        scan(it, t - 1)
                    elif not first:
                        scan(it - 1, GT - 1)
                    if t == 5 and not first:
                        add_skip(it - 1, (it - 1) & (DT_ - 1))

            dve.wait_ge(S["stk_zero"], 1)
            dve.wait_ge(S["brep_rd"], B)
            group(0, True)
            with dve.Fori(1, NG) as it:
                group(it, False)
            scan(NG - 1, GT - 1)
            add_skip(NG - 1, DT_ - 1)
            for k in range(B * CT):
                dve.wait_ge(S["op_ps"], k + 1)
                dve.tensor_scalar(XG[:, k // CT, k % CT], pair(k), CLAMP, -CLAMP, ALU.min, ALU.max).then_inc(S["op_rd"], 1)
            pixel_norm(1)
            dve.wait_ge(S["x1_rd"], B * CT)
            group_norm(1, XG2)
            dve.wait_ge(S["bn_ln"], 2)
            dve.tensor_tensor(INV[:, :], INV[:, :], BNG, ALU.mult).then_inc(S["bn_self"], 1)
            dve.wait_ge(S["bn_self"], 1)
            dve.tensor_tensor(SHF[:, :], BNM, INV[:, :], ALU.mult).then_inc(S["bn_self"], 1)
            dve.wait_ge(S["bn_self"], 2)
            dve.tensor_tensor(SHF[:, :], BNB, SHF[:, :], ALU.subtract).then_inc(S["bn_rd"], 1)
            dve.wait_ge(S["bn_rd"], 1)

            for b in range(B):
                for t in range(2):
                    dve.wait_ge(S["pad_rd"], QT * b + t + 1)
                    dve.tensor_scalar(QR[:, t].rearrange("p (y x) -> p y x", x=HW), PADB[:, b, t, PAD:PAD + HW, PAD:PAD + HW], 0.0, None, ALU.max).then_inc(S["q_rd"], 1)
                for t in range(QT):
                    n = QT * b + t
                    dve.wait_ge(S["pad_rd"], n + 1)
                    if n >= 2:
                        dve.wait_ge(S["cv_ps"], n - 1)
                    for i in range(DV_TAPS):
                        dy, dx = divmod(PE_TAPS + i, 5)
                        win, w = PADB[:, b, t, dy:dy + HW, dx:dx + HW], DW[:, t, PE_TAPS + i:PE_TAPS + i + 1]
                        if i == 0:
                            ins = dve.tensor_scalar(ACC[:, n % 2], win, w, None, ALU.mult)
                        else:
                            dve.wait_ge(S["acc_self"], (DV_TAPS - 1) * n + i)
                            ins = dve.scalar_tensor_tensor(out=ACC[:, n % 2], in0=win, scalar=w, in1=ACC[:, n % 2], op0=ALU.mult, op1=ALU.add)
                        ins.then_inc(S["acc_rd"] if i == DV_TAPS - 1 else S["acc_self"], 1)
                for w in range(4):
                    n = 4 * b + w
                    dve.wait_ge(S["vk_ps"], n + 1)
                    if n >= 2:
                        dve.wait_ge(S["nd_ps"], 2 * n - 2)
                    dve.tensor_copy(KS[:, n % 2:n % 2 + 1], PS[:, 6, P:P + 1]).then_inc(S["ks_rd"], 1)
                    dve.tensor_tensor(VKS[:, n % 2, 0, :], PS[:, 6, 0:P], MASK, ALU.mult).then_inc(S["vks_rd"], 1)
                    dve.wait_ge(S["ks_rd"], n + 1)
                    dve.tensor_scalar(VKS[:, n % 2, 1, :], MASK, KS[:, n % 2:n % 2 + 1], None, ALU.mult).then_inc(S["vks_rd"], 1)
                    dve.wait_ge(S["nd_ps"], 2 * n + 2)
                    dve.tensor_scalar(TMP[:, 0], pair(1), EPS_ATT, None, ALU.add).then_inc(S["den_self"], 1)
                    dve.wait_ge(S["den_self"], 2 * n + 1)
                    dve.reciprocal(TMP[:, 0], TMP[:, 0]).then_inc(S["den_self"], 1)
                    dve.wait_ge(S["den_self"], 2 * n + 2)
                    dve.tensor_tensor(QR[:, w], pair(0), TMP[:, 0], ALU.mult).then_inc(S["o_rd"], 1)
                for m in range(CT):
                    dve.wait_ge(S["pr_ps"], CT * b + m + 1)
                    dve.tensor_scalar(X[:, b, m], X[:, b, m], SHF[:, m:m + 1], None, ALU.add).then_inc(S["bn_rd"], 1)
                    dve.wait_ge(S["bn_rd"], CT * b + m + 2)
                    dve.scalar_tensor_tensor(out=X[:, b, m], in0=pair(m), scalar=INV[:, m:m + 1], in1=X[:, b, m], op0=ALU.mult, op1=ALU.add).then_inc(S["pr_rd"], 1)


def constants():
    import numpy as np
    p = np.arange(P)
    same_head = (p[:, None] // HD == p[None, :] // HD).astype(np.float32)
    cst = np.zeros((P, 6, P), np.float32)
    cst[:, 0] = same_head / HD
    cst[:, 1] = 1.0 / C
    cst[:, 2] = np.eye(P, dtype=np.float32)
    for n in range(NS):
        cst[R + n, 3, n::NS] = 1.0
        cst[R + NS + n, 4, n::NS] = 1.0
    cst[:, 5] = same_head
    selr = np.zeros((P, 4, 32), np.float32)
    selb = np.zeros((P, 4, P), np.float32)
    for j in range(4):
        for d in range(OCT):
            selr[d * NS:(d + 1) * NS, j, OCT * j + d] = 1.0
            for i in range(PARTS + 1):
                selb[32 * i + OCT * j + d, j, d * NS:(d + 1) * NS] = 1.0
    return cst, selr, selb


def kernel(**inputs):
    import numpy as _np
    import concourse.bacc as _bacc
    from concourse import mybir as _mybir
    from concourse.bass_utils import run_bass_kernel_spmd as _run

    v = {n.replace("L0_conv_", "a_").replace("L1_conv_", "b_"): _np.asarray(t) for n, t in inputs.items()}
    by_tile = lambda t: t.reshape(-1, P).T
    by_role = lambda t: t.reshape(C // HD, 3, HD, -1).swapaxes(0, 1).reshape(QC, -1)
    cst, selr, selb = constants()
    cols = _np.concatenate([
        by_tile(v["a_norm_w"]), by_tile(v["a_norm_b"]),
        v["a_conv_w"].reshape(DT_, P, KC).swapaxes(0, 1).reshape(P, DT_ * KC),
        by_tile(v["a_conv_b"]), by_tile(v["a_dt_proj_b"]), by_tile(v["a_D"]),
        by_tile(v["b_bn_gamma"]), by_tile(v["b_bn_beta"]), by_tile(v["b_bn_mean"]), by_tile(v["b_bn_var"])], axis=1)
    laid = {
        "x": v["x"].reshape(B, C, L),
        "win": v["a_in_proj_w"].T, "xpw": v["a_x_proj_w"].T, "dtw": v["a_dt_proj_w"].T,
        "alogr": v["a_A_log"], "alog": v["a_A_log"].reshape(DI // OCT, P).T, "wout": v["a_out_proj_w"].T,
        "wq": by_role(v["b_qkv_w"]).T, "wpr": v["b_proj_w"].T,
        "dw": by_role(v["b_dw_w"]),
        "pw": v["b_pw_w"].reshape(C // HD, 3, HD, HD).transpose(1, 0, 3, 2).reshape(QC, HD),
        "cols": cols, "cst": cst, "selr": selr, "selb": selb.astype(_mybir.dt.np(BF16)),
    }
    nc = _bacc.Bacc("TRN2", target_bir_lowering=False, num_devices=1)
    arrays, args = {}, {}
    for name, t in laid.items():
        t = _np.ascontiguousarray(t)
        arrays[f"in_{name}"] = t
        args[name] = nc.dram_tensor(f"in_{name}", t.shape, _mybir.dt.from_np(t.dtype), kind="ExternalInput").ap()
    out = nc.dram_tensor("out_0", (B, C, L), F32, kind="ExternalOutput").ap()
    mamba_attention_kernel(nc, args, out)
    r = _run(nc, [arrays], core_ids=[0])
    return r.results[0]["out_0"].reshape(B, C, HW, HW)
```

```python
from contextlib import ExitStack

import concourse.bass as bass
from concourse import mybir

ALU = mybir.AluOpType
ACT = mybir.ActivationFunctionType
F32 = mybir.dt.float32
BF16 = mybir.dt.bfloat16

P = 128
B = 2
C = 256
CT = C // P
HW = 32
L = HW * HW
HALF = 512
DI = 512
DT_ = DI // P
NS = 16
R = 16
XD = R + 2 * NS
KC = 4
OCT = P // NS
GT = P // OCT
NG = B * DT_
PARTS = 3
QC = 3 * C
QT = QC // P
HD = 8
PAD = 2
PW = HW + 2 * PAD
TAPS = 25
PE_TAPS = 6
POOL_TAPS = 5
DV_TAPS = TAPS - PE_TAPS - POOL_TAPS
BLK = L // P
ORDER = (2, 3, 4, 5, 0, 1)
CAP = 2.0
LOG_A_CAP = 20.0
CLAMP = 10.0
EPS = 1e-5
EPS_ATT = 1e-15


def mamba_attention_kernel(nc, a, out):
    with ExitStack() as ctx:
        def sb(name, shape, dt=F32):
            return ctx.enter_context(nc.sbuf_tensor(name, shape, dt))

        def sem(name):
            return ctx.enter_context(nc.semaphore(name))

        X = sb("X", [P, B, CT, L])[:, :, :, :]
        arena = sb("arena", [P, 20480])
        mid = sb("mid", [P, 20480])

        def view(t, at, *shape):
            n = 1
            for s in shape:
                n *= s
            names = "abcd"[:len(shape)]
            pat = f"p ({' '.join(names)}) -> p {' '.join(names)}"
            return t[:, at:at + n].rearrange(pat, **dict(zip(names, shape)))

        XG = view(arena, 0, B, CT, L)
        SQ = view(arena, 4096, B, CT, L)
        RS = view(arena, 8192, B, L)
        XIN = view(arena, 10240, 2, L + KC)
        CA = view(arena, 12296, 2, L)
        XDB = view(arena, 17408, B, L)
        DTF = view(arena, 0, 2, L)
        VV = view(arena, 2048, 2, L)
        DXF = view(arena, 4096, 2, L)
        DTR, DXR = arena[:, 6144:7168], arena[:, 7168:8192]
        dt_parts = arena[:, 8192:12288].bitcast(BF16).rearrange("p (r i l) -> p r i l", r=2, i=PARTS + 1)
        dx_parts = arena[:, 12288:15360].bitcast(BF16).rearrange("p (r i l) -> p r i l", r=2, i=PARTS)
        HT = arena[:, 15360:16384].bitcast(BF16).rearrange("p (r l) -> p r l", r=2)
        UM1 = arena[:, 19456:20480]

        def high(t):
            return t.bitcast(BF16).rearrange("p (l h) -> p l h", h=2)[:, :, 1]

        H = view(arena, 0, 4, L)
        G = view(arena, 4096, 8, L)
        stack = arena[:, 12288:20480].bitcast(BF16).rearrange("p (s k q l) -> p s k q l", s=2, k=2, q=4)
        XC = view(mid, 0, NG, L)
        SZ = view(mid, 8192, NG, L)
        BR = view(mid, 16384, B, L)
        CR = view(mid, 18432, B, L)
        PADB = arena[:, 0:B * QT * PW * PW].rearrange("p (b t y x) -> p b t y x", b=B, t=QT, y=PW)
        WT = view(arena, 15552, 2, PE_TAPS, P)
        ACC = view(arena, 18432, 2, HW, HW)
        SUM1 = view(arena, 17408, HW, HW)
        XG2 = view(mid, 0, B, CT, L)
        QR = (view(mid, 4096, 4, L), view(mid, 0, 4, L))
        KT = view(mid, 8192, BLK, 4, P)
        VT = view(mid, 12288, BLK, 4, P + 1)
        TMP = view(mid, 16416, 2, L)
        PROD = view(mid, 18464, HW, HW)
        DEN0 = mid[:, 19488:19488 + HALF]

        WIN = sb("WIN", [P, CT, 2 * DI])
        LNB = WIN[:, :, :]
        WQ = WIN[:, :, 0:QC]
        WOUT = sb("WOUT", [P, DT_, C])[:, :, :]
        WPR = sb("WPR", [P, 4, C])
        XPW = sb("XPW", [P, DT_, XD])
        SUM0 = WOUT.rearrange("p t c -> p (t c)").rearrange("p (y x) -> p y x", x=HW)
        PSUMS = (SUM0, SUM1)
        DTW = sb("DTW", [P, DI])
        VKS = [t.rearrange("p (i c) -> p i c", c=P) for t in (WIN[:, 0, QC:], WIN[:, 1, QC:], DTW[:, 0:2 * P], DTW[:, 2 * P:])]
        cst = sb("cst", [P, 6, P])
        GRP8, ONES, IDENT, REPB, REPC, MASK = (cst[:, i, :] for i in range(6))
        SELR = sb("SELR", [P, 4, 32])
        SELB = sb("SELB", [P, 4, P], BF16)
        SELX = X.rearrange("p b t l -> p (b t l)").bitcast(BF16).rearrange("p (g q j n) -> p g q j n", g=DT_, q=4, j=4)
        ALR = SZ[96:P].rearrange("p e l -> p (e l)").rearrange("p (o j n) -> p o j n", o=DT_ * 4, j=4)
        AC = sb("AC", [P, DI // OCT])
        COLS = sb("COLS", [P, 40])
        NW, NB = COLS[:, 0:2], COLS[:, 2:4]
        CW = COLS[:, 4:20].rearrange("p (t k) -> p t k", k=KC)
        CB, DTB, DD = COLS[:, 20:24], COLS[:, 24:28], COLS[:, 28:32]
        BNG, BNB, BNM, BNV = (COLS[:, 32 + 2 * i:34 + 2 * i] for i in range(4))
        DW = sb("DW", [P, QT, TAPS])
        PWN = sb("PWN", [P, QT, HD])
        PWB = sb("PWB", [P, QT, P])
        ST = sb("ST", [P, 4, 2, 6])
        MV = sb("MV", [P, 4, 2])
        GM = sb("GM", [P, 4])
        GV = sb("GV", [P, 4])
        GR = sb("GR", [P, 4])
        EPSC = sb("EPSC", [P, 1])
        EPSA = sb("EPSA", [P, 1])
        INV = sb("INV", [P, 2])
        SHF = sb("SHF", [P, 2])
        KS = sb("KS", [P, 4])
        PS = ctx.enter_context(nc.psum_tensor("PS", [P, 8, HALF], F32))

        def pair(k):
            return PS[:, 2 * k:2 * k + 2, :].rearrange("p a b -> p (a b)")

        def bank(k, c):
            return PS[:, 2 * k + c, :]

        def den_slot(u):
            return DEN0 if u < 8 else TMP[:, u % 2, 0:HALF]

        def attend_pair(u):
            return 1 if u >= 8 and u % 2 else 2

        def tap(b, t, k, c=None):
            dy, dx = divmod(k, 5)
            y, rows = (dy, HW) if c is None else (dy + HW // 2 * c, HW // 2)
            return PADB[:, b, t, y:y + rows, dx:dx + HW]

        dt_scratch = nc.dram_tensor("dt_parts", (NG, PARTS + 1, P, L), BF16, kind="Internal").ap()
        dx_scratch = nc.dram_tensor("dx_parts", (NG, PARTS, P, L), BF16, kind="Internal").ap()

        names = """ld_x ld_c ld_w0 ld_w1 eps_set pad_set
            gn_stat gn_self gn_mu_ps gn_dev gn_v gn_var_ps gn_ln gn_rstd gn_out
            ln_mu_ps ln_cent ln_sq ln_var_ps ln_lnv ln_rstd ln_self ln_out
            ip_ps xin_rd conv_self conv_out xc_rd sz_rd
            xd_zero xd_ps xd_rd rep_ps brep_rd crep_rd
            dt_ps sp_abs sp_exp sp_ln um1_rd sp_corr sp_sum v_rd dt_rd dx_rd hi_rd dt_r dx_r mid_rd dt_lo dx_lo dxhi_rd dxmid_rd alr_le
            dt_st0 dt_st1 dx_st0 dx_st1 ld_sel ld_alr ld_x1 selx_rd ex_lim ex_rd hic_rd stk_zero stk_ld0 stk_ld1 a_exp a_rd
            bc_dt bc_dx da_rd u_rd scan_rd g_rd red_ps y_add y_rd
            op_ps op_rd x1_rd
            pwb_rd pad_zero bn_ln bn_self bn_rd qkv_ps pad_rd q_rd tr_ps kv_rd one_set
            wt_rd pool_first pool_prod pool_add acc_self acc_rd cv_ps cv_rd tmp_rd vk_ps ks_rd vks_rd nd_ps den_ln den_rd att_set o_rd pr_ps pr_rd st_out""".split()
        S = {n: sem(n) for n in names}
        dt_st = [S[f"dt_st{r}"] for r in range(2)]
        dx_st = [S[f"dx_st{r}"] for r in range(2)]
        stk_ld = [S["stk_ld0"], S["stk_ld1"]]
        TILE_PS = 1

        block = ctx.enter_context(nc.Block())
        n_w0 = 0

        def between(n, c):
            steps = {(1, 0): [("to_pixels", 4)], (2, 0): [("to_pixels", 5)], (3, 0): [("to_pixels", 6)],
                     (4, 0): [("to_pixels", 7)], (4, 1): [("states", 0)],
                     (5, 0): [("to_pixels", 8), ("attend", 0)], (5, 1): [("to_pixels", 9), ("attend", 1), ("to_pixels", 10)],
                     (6, 0): [("to_pixels", 11), ("attend", 2)], (6, 1): [("attend", 3)],
                     (7, 0): [("attend", 4)], (7, 1): [("attend", 5), ("to_pixels", 12)],
                     (8, 0): [("attend", 6)], (8, 1): [("attend", 7), ("to_pixels", 13)],
                     (9, 0): [("project", 0)], (9, 1): [("project", 1), ("to_pixels", 14)],
                     (10, 0): [("project", 2), ("to_pixels", 15)], (10, 1): [("project", 3), ("states", 1)],
                     (11, 0): [("attend", 8), ("attend", 9)],
                     (11, 1): [("attend", u) for u in range(10, 16)] + [("project", p) for p in range(4, 8)]}
            return steps.get((n, c), [])

        @block.sync
        def _(sp):
            for b in range(B):
                sp.dma_start(X[:, b], a["x"][b].rearrange("(t p) l -> p t l", p=P)).then_inc(S["ld_x"], 16)
            sp.dma_start(ALR, a["alogr"].rearrange("(z c) n -> z (c n)", z=1).broadcast_to([32, DI * NS])
                         .rearrange("p (o j n) -> p o j n", o=DT_ * 4, j=4)).then_inc(S["ld_alr"], 16)
            sp.dma_start(WIN[:, :, :], a["win"].rearrange("(t p) n -> p t n", p=P)).then_inc(S["ld_w0"], 16)
            sp.dma_start(XPW[:, :, :], a["xpw"].rearrange("(t p) n -> p t n", p=P)).then_inc(S["ld_w0"], 16)
            sp.wait_ge(S["pad_set"], 2)
            sp.dma_start(DTW[0:R, :], a["dtw"]).then_inc(S["ld_w0"], 16)
            sp.dma_start(AC[:, :], a["alog"]).then_inc(S["ld_w0"], 16)
            sp.dma_start(WOUT[:, :, :], a["wout"].rearrange("(t p) n -> p t n", p=P)).then_inc(S["ld_w0"], 16)
            sp.dma_start(WPR[:, :, :], a["wpr"].rearrange("(t p) n -> p t n", p=P)).then_inc(S["ld_w0"], 16)
            sp.dma_start(DW[:, :, :], a["dw"].rearrange("(t p) n -> p t n", p=P)).then_inc(S["ld_w0"], 16)
            sp.dma_start(PWN[:, :, :], a["pw"].rearrange("(t p) n -> p t n", p=P)).then_inc(S["ld_w0"], 16)
            sp.wait_ge(S["gn_out"], 4)
            for o in range(DT_ * 4):
                sp.dma_start(SELX[0:96, o // 4, o % 4], a["selb"][0:96]).then_inc(S["ld_sel"], 16)
            for e in range(NG):
                for part in ("hic_rd", "mid_rd", "dt_lo"):
                    sp.wait_ge(S[part], e + 1)
                sp.dma_start(dt_scratch[e].rearrange("i p l -> p i l"), dt_parts[:, e % 2]).then_inc(dt_st[e % 2], 16)
                for part in ("dxhi_rd", "dxmid_rd", "dx_lo"):
                    sp.wait_ge(S[part], e + 1)
                sp.dma_start(dx_scratch[e].rearrange("i p l -> p i l"), dx_parts[:, e % 2]).then_inc(dx_st[e % 2], 16)
            for r in range(2):
                sp.wait_ge(dt_st[r], 16 * NG // 2)
                sp.wait_ge(dx_st[r], 16 * NG // 2)
            sp.wait_ge(S["stk_zero"], 1)

            def load_stack(e, s, n):
                for k, scratch in enumerate((dt_scratch, dx_scratch)):
                    for i in range(PARTS + 1 - k):
                        sp.dma_start(stack[32 * i:32 * i + 32, s, k],
                                     scratch[e, i].rearrange("(q c) l -> c q l", c=32)).then_inc(stk_ld[s], 16)

            load_stack(0, 0, 0)
            load_stack(1, 1, 0)
            with sp.Fori(1, NG // 2) as n:
                for s in range(2):
                    sp.wait_ge(S["bc_dt"], 16 * (2 * n + s) - 16)
                    load_stack(2 * n + s, s, n)
            sp.wait_ge(S["dt_rd"], NG)
            sp.dma_start(WQ, a["wq"].rearrange("(t p) n -> p t n", p=P)).then_inc(S["ld_w1"], 16)
            sp.wait_ge(S["bc_dt"], GT * NG)
            for b in range(B):
                sp.dma_start(X[:, b], a["x"][b].rearrange("(t p) l -> p t l", p=P)).then_inc(S["ld_x1"], 16)
            for b in range(B):
                for m in range(CT):
                    sp.wait_ge(S["pr_rd"], 4 * b + 2 * m + 2)
                    sp.dma_start(out[b, m * P:(m + 1) * P, :], X[:, b, m]).then_inc(S["st_out"], 16)
            sp.wait_ge(S["st_out"], 16 * B * CT)

        @block.gpsimd
        def _(pool):
            pool.memset(EPSC[:, :], EPS).then_inc(S["eps_set"], 1)
            pool.memset(EPSA[:, :], EPS_ATT).then_inc(S["eps_set"], 1)
            pool.memset(XIN[:, :, 0:KC - 1], 0.0).then_inc(S["pad_set"], 1)
            pool.memset(DTW[:, :], 0.0).then_inc(S["pad_set"], 1)
            pool.memset(XDB[:, :, :], 0.0).then_inc(S["xd_zero"], 1)
            pool.wait_ge(S["eps_set"], 2)
            pool.wait_ge(S["pad_set"], 2)
            pool.wait_ge(S["xd_zero"], 1)
            pool.wait_ge(S["ld_alr"], 16)
            pool.tensor_scalar(ALR, ALR, LOG_A_CAP, None, ALU.is_le).then_inc(S["alr_le"], 1)
            pool.wait_ge(S["alr_le"], 1)
            pool.wait_ge(S["ld_c"], 64)
            pool.wait_ge(S["gn_out"], 4)
            for j in range(4):
                pool.tensor_tensor(SELX[96:P].rearrange("p g q j n -> p (g q) j n")[:, :, j, :], ALR[:, :, j, :],
                                   SELB[96:P, j:j + 1, :].broadcast_to([32, DT_ * 4, P]), ALU.mult).then_inc(S["selx_rd"], 1)
            pool.wait_ge(S["ld_w0"], 128)
            pool.wait_ge(S["selx_rd"], 4)
            for t in range(QT):
                pool.tensor_tensor(PWB[:, t, :].rearrange("p (g o) -> p g o", o=HD),
                                   MASK.rearrange("p (g o) -> p g o", o=HD),
                                   PWN[:, t:t + 1, :].broadcast_to([P, P // HD, HD]), ALU.mult).then_inc(S["pwb_rd"], 1)
            for i in range(NG + 1):
                if i >= 1:
                    e = i - 1
                    if e >= 2:
                        pool.wait_ge(S["dxhi_rd"], e - 1)
                        pool.wait_ge(S["dx_r"], e - 1)
                    pool.wait_ge(S["dt_rd"], e + 1)
                    pool.tensor_tensor(DXF[:, e % 2], DTF[:, e % 2], XC[:, e], ALU.mult).then_inc(S["dx_rd"], 1)
                    if e >= 1:
                        pool.wait_ge(S["dxmid_rd"], e)
                        pool.wait_ge(S["dx_lo"], e)
                    pool.wait_ge(S["dx_rd"], e + 1)
                    pool.tensor_tensor(DXR, DXF[:, e % 2], high(DXF[:, e % 2]), ALU.subtract).then_inc(S["dx_r"], 1)
                    if e >= 2:
                        pool.wait_ge(dx_st[e % 2], 16 * (e // 2))
                    pool.wait_ge(S["dx_r"], e + 1)
                    pool.tensor_tensor(dx_parts[:, e % 2, 2], DXR, high(DXR), ALU.subtract).then_inc(S["dx_lo"], 1)
                if i < NG:
                    pool.wait_ge(S["sp_ln"], i + 1)
                    pool.wait_ge(S["um1_rd"], i + 1)
                    pool.tensor_tensor(LNB[:, i % 2], LNB[:, i % 2], UM1[:, :], ALU.subtract).then_inc(S["sp_corr"], 1)
            for r in range(2):
                pool.wait_ge(dt_st[r], 16 * NG // 2)
                pool.wait_ge(dx_st[r], 16 * NG // 2)
            pool.wait_ge(S["dt_ps"], NG)
            pool.wait_ge(S["sp_corr"], NG)
            pool.wait_ge(S["dx_lo"], NG)
            pool.memset(stack[96:P, :, 1], 0.0).then_inc(S["stk_zero"], 1)

            def mult_c(it, b, first):
                for t in range(GT):
                    pool.wait_ge(S["scan_rd"], GT * it + t + 1)
                    if not first or t >= 8:
                        pool.wait_ge(S["red_ps"], 4 * it + t // 4 - 1)
                    pool.tensor_tensor(G[:, t % 8], H[:, t % 4], CR[:, b], ALU.mult).then_inc(S["g_rd"], 1)
                    if t == 9 and not first:
                        gate(it - 1)

            def gate(it):
                pool.wait_ge(S["y_add"], it + 1)
                pool.wait_ge(S["sz_rd"], NG)
                pool.tensor_tensor(XC[:, it], XC[:, it], SZ[:, it], ALU.mult).then_inc(S["y_rd"], 1)

            pool.wait_ge(S["crep_rd"], B)
            pool.wait_ge(S["stk_zero"], 1)
            mult_c(0, 0, True)
            for b in range(B):
                with pool.Fori(max(1, b * DT_), (b + 1) * DT_) as it:
                    mult_c(it, b, False)
            gate(NG - 1)
            pool.wait_ge(S["x1_rd"], B * CT)
            images = PADB.rearrange("p b t y x -> p (b t) y x")
            for edge in (slice(0, PAD), slice(PAD + HW, PW)):
                pool.memset(images[:, :, edge, :], 0.0).then_inc(S["pad_zero"], 1)
                pool.memset(images[:, :, PAD:PAD + HW, edge], 0.0).then_inc(S["pad_zero"], 1)
            pool.wait_ge(S["op_ps"], B * CT)
            pool.memset(VT[:, :, :, P:P + 1], 1.0).then_inc(S["one_set"], 1)
            pool.wait_ge(S["red_ps"], 4 * NG)
            def tap_weights(n):
                if n >= 2:
                    pool.wait_ge(S["cv_ps"], 2 * n - 2)
                t = ORDER[n % QT]
                pool.tensor_tensor(WT[:, n % 2], PWB[:, t:t + 1, :].broadcast_to([P, PE_TAPS, P]),
                                   DW[:, t, 0:PE_TAPS].unsqueeze(2).broadcast_to([P, PE_TAPS, P]), ALU.mult).then_inc(S["wt_rd"], 1)

            tap_weights(0)
            tap_weights(1)
            for n in range(B * QT):
                b, t = n // QT, ORDER[n % QT]
                pool.wait_ge(S["pad_rd"], n + 1)
                if n >= 2:
                    pool.wait_ge(S["acc_self"], (DV_TAPS - 1) * (n - 2) + 1)
                for i in range(POOL_TAPS):
                    done = (POOL_TAPS - 1) * n + i
                    win, w = tap(b, t, PE_TAPS + i), DW[:, t, PE_TAPS + i:PE_TAPS + i + 1]
                    if i == 0:
                        pool.tensor_scalar(PSUMS[n % 2], win, w, 0.0, ALU.mult, ALU.add).then_inc(S["pool_first"], 1)
                        continue
                    if done - 1 >= 1:
                        pool.wait_ge(S["pool_add"], done - 1)
                    pool.tensor_scalar(PROD, win, w, 0.0, ALU.mult, ALU.add).then_inc(S["pool_prod"], 1)
                    pool.wait_ge(S["pool_prod"], done)
                    pool.wait_ge(S["pool_first"], n + 1)
                    pool.tensor_tensor(PSUMS[n % 2], PSUMS[n % 2], PROD, ALU.add).then_inc(S["pool_add"], 1)
                if n >= 2:
                    tap_weights(n)

        @block.scalar
        def _(act):
            act.dma_start(cst[:, :, :], a["cst"]).then_inc(S["ld_c"], 16)
            act.dma_start(SELR[:, :, :], a["selr"]).then_inc(S["ld_c"], 16)
            act.dma_start(SELB[:, :, :], a["selb"]).then_inc(S["ld_c"], 16)
            act.dma_start(COLS[:, :], a["cols"]).then_inc(S["ld_c"], 16)
            act.wait_ge(S["eps_set"], 2)

            def group_rstd(ph):
                act.wait_ge(S["gn_var_ps"], ph + 1)
                act.activation(GR[:, :], PS[:, 1, 0:4], ACT.Ln, bias=EPSC[:, :]).then_inc(S["gn_ln"], 1)
                act.wait_ge(S["gn_ln"], ph + 1)
                act.activation(GR[:, :], GR[:, :], ACT.Exp, scale=-0.5).then_inc(S["gn_rstd"], 1)

            def pixel_rstd(ph):
                for b in range(B):
                    n = B * ph + b
                    for t in range(CT):
                        act.wait_ge(S["ln_cent"], CT * n + t + 1)
                        act.activation(SQ[:, b, t], XG[:, b, t], ACT.Square).then_inc(S["ln_sq"], 1)
                    act.wait_ge(S["ln_var_ps"], n + 1)
                    act.activation(RS[:, b], pair(2 + b), ACT.Ln, bias=EPSC[:, :]).then_inc(S["ln_lnv"], 1)
                    act.wait_ge(S["ln_lnv"], n + 1)
                    act.activation(RS[:, b], RS[:, b], ACT.Exp, scale=-0.5).then_inc(S["ln_rstd"], 1)

            group_rstd(0)
            act.wait_ge(S["ld_w0"], 128)
            act.activation(AC[:, :], AC[:, :], ACT.Exp).then_inc(S["a_exp"], 1)
            pixel_rstd(0)

            def silu_xc(e):
                act.wait_ge(S["conv_out"], e + 1)
                act.activation(XC[:, e], CA[:, e % 2], ACT.Silu, bias=CB[:, e % DT_:e % DT_ + 1]).then_inc(S["xc_rd"], 1)

            act.wait_ge(S["pad_set"], 2)
            for b in range(B):
                for m in range(2 * DT_):
                    k = 2 * DT_ * b + m
                    act.wait_ge(S["ip_ps"], k + 1)
                    if m < DT_:
                        e = DT_ * b + m
                        if e >= 2:
                            act.wait_ge(S["conv_out"], e - 1)
                            act.wait_ge(S["xc_rd"], e - 1)
                        act.activation(XIN[:, e % 2, KC - 1:KC - 1 + L], pair(k % 4), ACT.Copy).then_inc(S["xin_rd"], 1)
                        act.activation(CA[:, e % 2], pair(k % 4), ACT.Copy, scale=CW[:, m, KC - 1:KC]).then_inc(S["xin_rd"], 1)
                    else:
                        if k == DT_:
                            act.wait_ge(S["selx_rd"], 4)
                        act.activation(SZ[:, DT_ * b + m - DT_], pair(k % 4), ACT.Silu).then_inc(S["sz_rd"], 1)
                    if 1 <= m <= DT_:
                        silu_xc(DT_ * b + m - 1)
            for b in range(B):
                act.wait_ge(S["xd_ps"], b + 1)
                act.wait_ge(S["xd_zero"], 1)
                act.activation(XDB[0:XD, b], pair(b)[0:XD, :], ACT.Copy).then_inc(S["xd_rd"], 1)
            for b in range(B):
                act.wait_ge(S["rep_ps"], 2 * b + 2)
                act.activation(CR[:, b], pair(2 * b + 1), ACT.Copy).then_inc(S["crep_rd"], 1)

            for i in range(NG + 1):
                if i < NG:
                    if i >= 2:
                        act.wait_ge(S["dx_rd"], i - 1)
                        act.wait_ge(S["dt_r"], i - 1)
                        act.wait_ge(S["hi_rd"], i - 1)
                    act.wait_ge(S["v_rd"], i + 1)
                    act.activation(DTF[:, i % 2], VV[:, i % 2], ACT.Abs).then_inc(S["sp_abs"], 1)
                    act.wait_ge(S["sp_abs"], i + 1)
                    act.activation(DTF[:, i % 2], DTF[:, i % 2], ACT.Exp, scale=-1.0).then_inc(S["sp_exp"], 1)
                    if i >= 2:
                        act.wait_ge(S["sp_sum"], i - 1)
                    act.wait_ge(S["sp_exp"], i + 1)
                    act.activation(LNB[:, i % 2], DTF[:, i % 2], ACT.Ln, bias=1.0).then_inc(S["sp_ln"], 1)
                if i >= 1:
                    e = i - 1
                    if e >= 2:
                        act.wait_ge(S["hic_rd"], e - 1)
                    act.wait_ge(S["dt_rd"], e + 1)
                    act.activation(HT[:, e % 2], high(DTF[:, e % 2]), ACT.Copy).then_inc(S["hi_rd"], 1)
                    if e >= 2:
                        act.wait_ge(dt_st[e % 2], 16 * (e // 2))
                        act.wait_ge(dx_st[e % 2], 16 * (e // 2))
                    act.wait_ge(S["dt_r"], e + 1)
                    act.activation(dt_parts[:, e % 2, 1], high(DTR), ACT.Copy).then_inc(S["mid_rd"], 1)
                    act.wait_ge(S["dx_rd"], e + 1)
                    act.activation(dx_parts[:, e % 2, 0], high(DXF[:, e % 2]), ACT.Copy).then_inc(S["dxhi_rd"], 1)
                    act.wait_ge(S["dx_r"], e + 1)
                    act.activation(dx_parts[:, e % 2, 1], high(DXR), ACT.Copy).then_inc(S["dxmid_rd"], 1)
            act.wait_ge(S["a_rd"], 1)
            with act.Fori(0, NG) as it:
                g = it & (DT_ - 1)
                for t in range(GT):
                    act.wait_ge(S["bc_dt"], GT * it + t + 1)
                    octave = GT * g + 4 * (t % 4) + t // 4
                    act.activation(pair(t % 2), pair(t % 2), ACT.Exp, scale=AC[:, bass.ds(octave, 1)]).then_inc(S["da_rd"], 1)
            pixel_rstd(1)
            group_rstd(1)
            act.activation(INV[:, :], BNV, ACT.Ln, bias=EPSC[:, :]).then_inc(S["bn_ln"], 1)
            act.wait_ge(S["bn_ln"], 1)
            act.activation(INV[:, :], INV[:, :], ACT.Exp, scale=-0.5).then_inc(S["bn_ln"], 1)

            def copy_kv_qkv(i):
                b, j = divmod(i, 8)
                act.wait_ge(S["pad_rd"], QT * b + j + 1)
                if i >= 2:
                    act.wait_ge(S["tr_ps"], i - 1)
                act.activation(TMP[:, i % 2].rearrange("p (y x) -> p y x", x=HW), PADB[:, b, 2 + j, PAD:PAD + HW, PAD:PAD + HW],
                               ACT.Copy).then_inc(S["tmp_rd"], 2)

            def evac_kv(i):
                b, w = divmod(i, 8)
                act.wait_ge(S["tr_ps"], i + 1)
                path, j = divmod(w, 4)
                src = pair(3).rearrange("p (k c) -> p k c", c=P)
                if w == 0 and b:
                    act.wait_ge(S["vk_ps"], 4 * b)
                if j < 2:
                    act.activation(KT[:, :, 2 * path + j, :], src, ACT.Relu).then_inc(S["kv_rd"], 1)
                else:
                    act.activation(VT[:, :, 2 * path + j - 2, 0:P], src, ACT.Copy).then_inc(S["kv_rd"], 1)

            def reciprocal(u):
                act.wait_ge(S["nd_ps"], 2 * u + 2)
                if 1 <= u < 8:
                    act.wait_ge(S["o_rd"], u)
                elif u >= 10:
                    act.wait_ge(S["o_rd"], u - 1)
                elif u >= 8:
                    act.wait_ge(S["tr_ps"], 8 * B)
                act.activation(den_slot(u), bank(attend_pair(u), 1), ACT.Ln, bias=EPSA[:, :]).then_inc(S["den_ln"], 1)
                act.wait_ge(S["den_ln"], u + 1)
                act.activation(den_slot(u), den_slot(u), ACT.Exp, scale=-1.0).then_inc(S["den_rd"], 1)

            def act_between(n, c):
                for what, i in between(n, c):
                    if what == "to_pixels":
                        evac_kv(i)
                        if i == 7:
                            copy_kv_qkv(8)
                            copy_kv_qkv(9)
                        elif i in (8, 9):
                            copy_kv_qkv(i + 2)
                    elif what == "attend":
                        reciprocal(i)

            act.wait_ge(S["one_set"], 1)
            act.wait_ge(S["pad_zero"], 4)
            for k in range(B * QT):
                b, j = divmod(k, QT)
                act.wait_ge(S["qkv_ps"], k + 1)
                act.activation(PADB[:, b, ORDER[j], PAD:PAD + HW, PAD:PAD + HW],
                               pair(k % 2 * 2).rearrange("p (y x) -> p y x", x=HW), ACT.Copy).then_inc(S["pad_rd"], 1)
                if k in (1, 2, 3):
                    copy_kv_qkv(k - 1)
                    if k >= 2:
                        evac_kv(k - 2)
                elif k == 4:
                    copy_kv_qkv(3)
                    evac_kv(2)
                elif k == 5:
                    evac_kv(3)
            act.wait_ge(S["pad_rd"], B * QT)
            for b in range(B):
                for t in range(2):
                    act.activation(QR[b][:, t].rearrange("p (y x) -> p y x", x=HW), PADB[:, b, t, PAD:PAD + HW, PAD:PAD + HW],
                                   ACT.Relu).then_inc(S["q_rd"], 1)
            for n in range(B * QT):
                b, j = divmod(n, QT)
                for c in range(2):
                    act.wait_ge(S["cv_ps"], 2 * n + c + 1)
                    half = slice(c * HALF, (c + 1) * HALF)
                    if j < 4:
                        i = 8 * b + 4 + j
                        act.wait_ge(S["tr_ps"], i - 1)
                        act.activation(TMP[:, i % 2, half], bank(0, c), ACT.Copy).then_inc(S["tmp_rd"], 1)
                    else:
                        act.activation(QR[b][:, 2 + ORDER[j], half], bank(0, c), ACT.Relu).then_inc(S["cv_rd"], 1)
                    act_between(n, c)

        @block.tensor
        def _(pe):
            pe.wait_ge(S["ld_c"], 64)

            def group_stats(ph):
                pe.wait_ge(S["gn_stat"], 4 * (ph + 1))
                pe.matmul(PS[:, 0, 0:4], GRP8, MV[:, :, 0], start=True, stop=True).then_inc(S["gn_mu_ps"], 1)
                pe.wait_ge(S["gn_v"], ph + 1)
                pe.matmul(PS[:, 1, 0:4], GRP8, GV[:, :], start=True, stop=True).then_inc(S["gn_var_ps"], 1)

            def pixel_stats(ph, ready, count):
                for b in range(B):
                    pe.wait_ge(ready, count * (b + 1))
                    for c in range(2):
                        for t in range(CT):
                            mm = pe.matmul(bank(b, c), ONES, XG[:, b, t, c * HALF:(c + 1) * HALF], start=(t == 0), stop=(t == CT - 1))
                    mm.then_inc(S["ln_mu_ps"], 1)
                for b in range(B):
                    pe.wait_ge(S["ln_sq"], CT * (B * ph + b + 1))
                    for c in range(2):
                        for t in range(CT):
                            mm = pe.matmul(bank(2 + b, c), ONES, SQ[:, b, t, c * HALF:(c + 1) * HALF], start=(t == 0), stop=(t == CT - 1))
                    mm.then_inc(S["ln_var_ps"], 1)

            group_stats(0)
            pe.wait_ge(S["gn_rstd"], 1)
            pe.wait_ge(S["gn_dev"], 1)
            pixel_stats(0, S["gn_out"], CT)
            pe.wait_ge(S["ld_w0"], 128)
            for b in range(B):
                pe.wait_ge(S["ln_out"], CT * (b + 1))
                for m in range(2 * DT_):
                    k = 2 * DT_ * b + m
                    if k < 2:
                        pe.wait_ge(S["ln_cent"], CT * (k + 1))
                    elif k < 4:
                        pe.wait_ge(S["ln_lnv"], k - 1)
                    else:
                        kb, km = divmod(k - 4, 2 * DT_)
                        if km < DT_:
                            pe.wait_ge(S["xin_rd"], 2 * (DT_ * kb + km + 1))
                        else:
                            pe.wait_ge(S["sz_rd"], DT_ * kb + km - DT_ + 1)
                    for c in range(2):
                        for t in range(CT):
                            mm = pe.matmul(bank(k % 4, c), WIN[:, t, m * P:(m + 1) * P], XG[:, b, t, c * HALF:(c + 1) * HALF], start=(t == 0), stop=(t == CT - 1))
                    mm.then_inc(S["ip_ps"], 1)
            pe.wait_ge(S["sz_rd"], NG)
            for b in range(B):
                pe.wait_ge(S["xc_rd"], DT_ * (b + 1))
                for c in range(2):
                    for t in range(DT_):
                        mm = pe.matmul(bank(b, c)[0:XD, :], XPW[:, t, :], XC[:, DT_ * b + t, c * HALF:(c + 1) * HALF], start=(t == 0), stop=(t == DT_ - 1))
                mm.then_inc(S["xd_ps"], 1)
            for b in range(B):
                pe.wait_ge(S["xd_rd"], B)
                for i, rep in enumerate((REPB, REPC)):
                    for c in range(2):
                        mm = pe.matmul(bank(2 * b + i, c), rep, XDB[:, b, c * HALF:(c + 1) * HALF], start=True, stop=True)
                    mm.then_inc(S["rep_ps"], 1)
            pe.wait_ge(S["pad_set"], 2)
            for e in range(NG):
                if e < 4:
                    pe.wait_ge(S["brep_rd"] if e % 2 == 0 else S["crep_rd"], e // 2 + 1)
                else:
                    pe.wait_ge(S["v_rd"], e - 3)
                for c in range(2):
                    mm = pe.matmul(bank(e % 4, c), DTW[:, (e % DT_) * P:(e % DT_ + 1) * P], XDB[:, e // DT_, c * HALF:(c + 1) * HALF], start=True, stop=True)
                mm.then_inc(S["dt_ps"], 1)
            pe.wait_ge(S["v_rd"], NG)

            def spread(it, g, s, t, first):
                if t == 0:
                    pe.wait_ge(stk_ld[s], 112 * ((it >> 1) + 1))
                if not first or t >= 1:
                    pe.wait_ge(S["u_rd"], GT * it + t)
                for c in range(2):
                    mm = pe.matmul(bank(2, c), SELX[:, g, t % 4, t // 4, :], stack[:, s, 1, t % 4, c * HALF:(c + 1) * HALF], start=True, stop=True)
                mm.then_inc(S["bc_dx"], 1)
                if not first or t >= 2:
                    pe.wait_ge(S["scan_rd"], GT * it + t - 1)
                for c in range(2):
                    mm = pe.matmul(bank(t % 2, c), SELX[:, g, t % 4, t // 4, :], stack[:, s, 0, t % 4, c * HALF:(c + 1) * HALF], start=True, stop=True)
                mm.then_inc(S["bc_dt"], 1)

            def state_sum(it, k, c, first):
                if c == 0:
                    pe.wait_ge(S["g_rd"], GT * it + 4 * k + 4)
                if k == 0 and c == 0 and not first:
                    pe.wait_ge(S["y_add"], it)
                for q in range(4):
                    mm = pe.matmul(bank(3, c)[32 * q:32 * q + 32, :], SELR[:, k, :], G[:, (4 * k + q) % 8, c * HALF:(c + 1) * HALF],
                                   start=(k == 0), stop=(k == 3))
                if c:
                    mm.then_inc(S["red_ps"], 1)

            def group(it, s, first):
                g = 0 if first else it & (DT_ - 1)
                for t in range(GT):
                    spread(it, g, s, t, first)
                    if t in (2, 3):
                        if not first:
                            state_sum(it - 1, 3, t - 2, False)
                    elif t % 4 >= 2:
                        state_sum(it, t // 4 - 1, t % 4 - 2, first)

            pe.wait_ge(S["ld_sel"], 16 * DT_ * 4)
            pe.wait_ge(S["selx_rd"], 4)
            group(0, 0, True)
            with pe.Fori(0, NG // 2 - 1) as n:
                group(2 * n + 1, 1, False)
                group(2 * n + 2, 0, False)
            group(NG - 1, 1, False)
            for c in range(2):
                state_sum(NG - 1, 3, c, False)
            for b in range(B):
                pe.wait_ge(S["y_rd"], DT_ * (b + 1))
                for m in range(CT):
                    k = CT * b + m
                    if b == 0 and m == 0:
                        pe.wait_ge(S["scan_rd"], GT * NG)
                        pe.wait_ge(S["u_rd"], GT * NG)
                        pe.wait_ge(S["y_add"], NG)
                    for c in range(2):
                        for t in range(DT_):
                            mm = pe.matmul(bank(k, c), WOUT[:, t, m * P:(m + 1) * P], XC[:, DT_ * b + t, c * HALF:(c + 1) * HALF], start=(t == 0), stop=(t == DT_ - 1))
                    mm.then_inc(S["op_ps"], 1)
            pe.wait_ge(S["op_rd"], B * CT)
            pixel_stats(1, S["op_rd"], CT)
            pe.wait_ge(S["ln_rstd"], 2 * B)
            pe.wait_ge(S["ln_cent"], 2 * B * CT)
            group_stats(1)
            pe.wait_ge(S["gn_rstd"], 2)
            pe.wait_ge(S["ld_w1"], 16)

            def to_pixels(i):
                pe.wait_ge(S["tmp_rd"], 2 * i + 2)
                if i >= 1:
                    pe.wait_ge(S["kv_rd"], i)
                if i == 8:
                    pe.wait_ge(S["vks_rd"], 8)
                    pe.wait_ge(S["ks_rd"], 4)
                for j in range(BLK):
                    mm = pe.transpose(bank(3, j // 4)[:, (j % 4) * P:(j % 4 + 1) * P], TMP[:, i % 2, j * P:(j + 1) * P], IDENT)
                mm.then_inc(S["tr_ps"], 1)

            def states(b):
                pe.wait_ge(S["kv_rd"], 8 * (b + 1))
                for w in range(4):
                    if w >= 2:
                        pe.wait_ge(S["vks_rd"], 8 * b + 2 * w - 2)
                        pe.wait_ge(S["ks_rd"], 4 * b + w - 1)
                    for j in range(BLK):
                        mm = pe.matmul(bank(3, w % 2)[:, 0:P + 1], KT[:, j, w, :], VT[:, j, w, :], start=(j == 0), stop=(j == BLK - 1))
                    mm.then_inc(S["vk_ps"], 1)

            def attend(u):
                b, i = divmod(u, 8)
                w, c = divmod(i, 2)
                pe.wait_ge(S["vks_rd"], 8 * b + 2 * w + 2)
                if w < 2:
                    pe.wait_ge(S["q_rd"], 2 * b + w + 1)
                else:
                    pe.wait_ge(S["cv_rd"], 2 * (2 * b + w - 2) + c + 1)
                if i == 0 and b:
                    pe.wait_ge(S["pr_rd"], 4 * b)
                if 1 <= u < 8:
                    pe.wait_ge(S["o_rd"], u)
                elif u >= 10:
                    pe.wait_ge(S["o_rd"], u - 1)
                for k in range(2):
                    pe.matmul(bank(attend_pair(u), k), VKS[w][:, k, :], QR[b][:, w, c * HALF:(c + 1) * HALF], start=True, stop=True).then_inc(S["nd_ps"], 1)

            def project(p):
                b, i = divmod(p, 4)
                m, c = divmod(i, 2)
                if i == 0:
                    pe.wait_ge(S["o_rd"], 8 * (b + 1))
                if i >= 2 and b == 0:
                    pe.wait_ge(S["pr_rd"], p - 1)
                for w in range(4):
                    mm = pe.matmul(bank(2 - m * b, c), WPR[:, w, m * P:(m + 1) * P], QR[b][:, w, c * HALF:(c + 1) * HALF], start=(w == 0), stop=(w == 3))
                mm.then_inc(S["pr_ps"], 1)

            pe_steps = {"to_pixels": to_pixels, "states": states, "attend": attend, "project": project}
            for k in range(B * QT):
                b, j = divmod(k, QT)
                t = ORDER[j]
                if j == 0:
                    pe.wait_ge(S["gn_out"], 4 + CT * (b + 1))
                if k >= 2:
                    pe.wait_ge(S["pad_rd"], k - 1)
                for c in range(2):
                    for u in range(CT):
                        mm = pe.matmul(bank(k % 2 * 2, c), WQ[:, u, t * P:(t + 1) * P], XG2[:, b, u, c * HALF:(c + 1) * HALF], start=(u == 0), stop=(u == CT - 1))
                mm.then_inc(S["qkv_ps"], 1)
                if 2 <= k <= 5:
                    to_pixels(k - 2)
            pe.wait_ge(S["pad_rd"], B * QT)
            for n in range(B * QT):
                b, j = divmod(n, QT)
                t = ORDER[j]
                pe.wait_ge(S["wt_rd"], n + 1)
                for c in range(2):
                    if n:
                        pb, pj = divmod(n - 1, QT)
                        if pj < 4:
                            pe.wait_ge(S["tmp_rd"], 2 * (8 * pb + 4 + pj) + c + 1)
                        else:
                            pe.wait_ge(S["cv_rd"], 2 * (2 * pb + pj - 4) + c + 1)
                    for k in range(PE_TAPS):
                        pe.matmul(bank(0, c), WT[:, n % 2, k, :], tap(b, t, k, c), start=(k == 0), stop=False)
                    pe.wait_ge(S["acc_rd"], n + 1)
                    pe.matmul(bank(0, c), PWB[:, t, :], ACC[:, n % 2, 16 * c:16 * c + 16, :], start=False, stop=True).then_inc(S["cv_ps"], 1)
                    for what, i in between(n, c):
                        pe_steps[what](i)

        @block.vector
        def _(dve):
            def group_norm(ph, dst):
                for i in range(4):
                    b, t = divmod(i, CT)
                    if ph == 0:
                        if t == 0:
                            dve.wait_ge(S["ld_x"], 32)
                    for c in range(2):
                        dve.bn_stats(ST[:, i, c, :], X[:, b, t, c * HALF:(c + 1) * HALF]).then_inc(S["gn_self"], 1)
                    dve.wait_ge(S["gn_self"], 14 * ph + 2 * i + 2)
                    dve.bn_aggr(MV[:, i, :], ST[:, i, :, :]).then_inc(S["gn_stat"], 1)
                dve.wait_ge(S["gn_mu_ps"], ph + 1)
                dve.tensor_copy(GM[:, :], PS[:, 0, 0:4]).then_inc(S["gn_self"], 1)
                dve.wait_ge(S["gn_self"], 14 * ph + 9)
                dve.tensor_tensor(GV[:, :], MV[:, :, 0], GM[:, :], ALU.subtract).then_inc(S["gn_dev"], 1)
                dve.wait_ge(S["gn_dev"], ph + 1)
                dve.tensor_tensor(GV[:, :], GV[:, :], GV[:, :], ALU.mult).then_inc(S["gn_self"], 1)
                dve.wait_ge(S["gn_self"], 14 * ph + 10)
                dve.tensor_tensor(GV[:, :], GV[:, :], MV[:, :, 1], ALU.add).then_inc(S["gn_v"], 1)
                dve.wait_ge(S["gn_rstd"], ph + 1)
                for i in range(4):
                    b, t = divmod(i, CT)
                    ins = dve.tensor_scalar(dst[:, b, t], X[:, b, t], GM[:, i:i + 1], GR[:, i:i + 1], ALU.subtract, ALU.mult)
                    if ph == 0:
                        ins.then_inc(S["gn_self"], 1)
                        dve.wait_ge(S["gn_self"], 11 + i)
                        ins = dve.tensor_scalar(dst[:, b, t], dst[:, b, t], CLAMP, -CLAMP, ALU.min, ALU.max)
                    ins.then_inc(S["gn_out"], 1)

            def pixel_norm(ph):
                for b in range(B):
                    n = B * ph + b
                    dve.wait_ge(S["ln_mu_ps"], n + 1)
                    for t in range(CT):
                        dve.tensor_tensor(XG[:, b, t], XG[:, b, t], pair(b), ALU.subtract).then_inc(S["ln_cent"], 1)
                for b in range(B):
                    n = B * ph + b
                    dve.wait_ge(S["ln_rstd"], n + 1)
                    for t in range(CT):
                        i = 2 * CT * b + 2 * t + 8 * ph
                        if ph == 1:
                            i = 8 + 2 * CT * b + 2 * t
                        dve.wait_ge(S["ln_cent"], CT * n + t + 1)
                        dve.tensor_tensor(XG[:, b, t], XG[:, b, t], RS[:, b], ALU.mult).then_inc(S["ln_self"], 1)
                        dve.wait_ge(S["ln_self"], i + 1)
                        if ph == 0:
                            dve.tensor_scalar(XG[:, b, t], XG[:, b, t], NW[:, t:t + 1], NB[:, t:t + 1], ALU.mult, ALU.add).then_inc(S["ln_self"], 1)
                            dve.wait_ge(S["ln_self"], i + 2)
                            dve.tensor_scalar(XG[:, b, t], XG[:, b, t], CLAMP, -CLAMP, ALU.min, ALU.max).then_inc(S["ln_out"], 1)
                        else:
                            dve.tensor_scalar(XG[:, b, t], XG[:, b, t], CLAMP, -CLAMP, ALU.min, ALU.max).then_inc(S["ln_self"], 1)
                            dve.wait_ge(S["ln_self"], i + 2)
                            dve.wait_ge(S["ld_x1"], 32)
                            dve.tensor_tensor(X[:, b, t], X[:, b, t], XG[:, b, t], ALU.add).then_inc(S["x1_rd"], 1)

            dve.wait_ge(S["ld_c"], 64)
            group_norm(0, XG)
            pixel_norm(0)
            dve.wait_ge(S["a_exp"], 1)
            dve.tensor_scalar(AC[:, :], AC[:, :], -1.0, None, ALU.mult).then_inc(S["a_rd"], 1)
            for e in range(NG):
                m = e % DT_
                dve.wait_ge(S["xin_rd"], 2 * e + 2)
                for k in range(KC - 1):
                    if k:
                        dve.wait_ge(S["conv_self"], 2 * e + k)
                    ins = dve.scalar_tensor_tensor(out=CA[:, e % 2], in0=XIN[:, e % 2, k:k + L], scalar=CW[:, m, k:k + 1], in1=CA[:, e % 2], op0=ALU.mult, op1=ALU.add)
                    ins.then_inc(S["conv_out"] if k == KC - 2 else S["conv_self"], 1)
            for b in range(B):
                dve.wait_ge(S["rep_ps"], 2 * b + 1)
                dve.tensor_copy(BR[:, b], pair(2 * b)).then_inc(S["brep_rd"], 1)

            for i in range(NG + 1):
                if i < NG:
                    dve.wait_ge(S["dt_ps"], i + 1)
                    if i >= 2:
                        dve.wait_ge(S["sp_abs"], i - 1)
                        dve.wait_ge(S["dt_rd"], i - 1)
                    dve.tensor_scalar(VV[:, i % 2], pair(i % 4), DTB[:, i % DT_:i % DT_ + 1], None, ALU.add).then_inc(S["v_rd"], 1)
                if i >= 1:
                    e = i - 1
                    dve.wait_ge(S["sp_corr"], e + 1)
                    dve.scalar_tensor_tensor(out=DTF[:, e % 2], in0=LNB[:, e % 2], scalar=0.0, in1=DTF[:, e % 2], op0=ALU.min, op1=ALU.add).then_inc(S["sp_sum"], 1)
                    dve.wait_ge(S["sp_sum"], e + 1)
                    dve.scalar_tensor_tensor(out=DTF[:, e % 2], in0=VV[:, e % 2], scalar=0.0, in1=DTF[:, e % 2], op0=ALU.max, op1=ALU.add).then_inc(S["dt_rd"], 1)
                    if e >= 1:
                        dve.wait_ge(S["mid_rd"], e)
                        dve.wait_ge(S["dt_lo"], e)
                    dve.wait_ge(S["dt_rd"], e + 1)
                    dve.tensor_tensor(DTR, DTF[:, e % 2], high(DTF[:, e % 2]), ALU.subtract).then_inc(S["dt_r"], 1)
                if i < NG:
                    if i >= 1:
                        dve.wait_ge(S["sp_corr"], i)
                    dve.wait_ge(S["sp_exp"], i + 1)
                    dve.tensor_scalar(UM1[:, :], DTF[:, i % 2], 1.0, 1.0, ALU.add, ALU.subtract).then_inc(S["um1_rd"], 1)
                if i >= 1:
                    if e >= 2:
                        dve.wait_ge(dt_st[e % 2], 16 * (e // 2))
                    dve.wait_ge(S["dt_r"], e + 1)
                    dve.tensor_tensor(dt_parts[:, e % 2, 2], DTR, high(DTR), ALU.subtract).then_inc(S["dt_lo"], 1)
                    dve.wait_ge(S["hi_rd"], e + 1)
                    dve.tensor_scalar(dt_parts[:, e % 2, 3], HT[:, e % 2], CAP, 0.0, ALU.subtract, ALU.max).then_inc(S["ex_lim"], 1)
                    dve.wait_ge(S["ex_lim"], e + 1)
                    dve.scalar_tensor_tensor(out=dt_parts[:, e % 2, 3], in0=HT[:, e % 2], scalar=63.0 / 64, in1=dt_parts[:, e % 2, 3],
                                             op0=ALU.mult, op1=ALU.min).then_inc(S["ex_rd"], 1)
                    dve.wait_ge(S["ex_rd"], e + 1)
                    dve.tensor_tensor(dt_parts[:, e % 2, 0], HT[:, e % 2], dt_parts[:, e % 2, 3], ALU.subtract).then_inc(S["hic_rd"], 1)

            def take_u(it, b, t, first):
                dve.wait_ge(S["bc_dx"], GT * it + t + 1)
                if not first or t >= 4:
                    dve.wait_ge(S["g_rd"], GT * it + t - 3)
                dve.tensor_tensor(H[:, t % 4], pair(2), BR[:, b], ALU.mult).then_inc(S["u_rd"], 1)

            def scan(it, t):
                dve.wait_ge(S["da_rd"], GT * it + t + 1)
                dve.wait_ge(S["u_rd"], GT * it + t + 1)
                dve.tensor_tensor_scan(H[:, t % 4], pair(t % 2), H[:, t % 4], 0.0, ALU.mult, ALU.add).then_inc(S["scan_rd"], 1)

            def add_skip(it, g):
                dve.wait_ge(S["red_ps"], 4 * it + 4)
                dve.scalar_tensor_tensor(out=XC[:, it], in0=XC[:, it], scalar=DD[:, bass.ds(g, 1)], in1=pair(3), op0=ALU.mult, op1=ALU.add).then_inc(S["y_add"], 1)

            def group(it, first):
                b = 0 if first else (it >> 2) & 1
                for t in range(GT):
                    take_u(it, b, t, first)
                    if t:
                        scan(it, t - 1)
                    elif not first:
                        scan(it - 1, GT - 1)
                    if t == 5 and not first:
                        add_skip(it - 1, (it - 1) & (DT_ - 1))

            dve.wait_ge(S["stk_zero"], 1)
            dve.wait_ge(S["brep_rd"], B)
            group(0, True)
            with dve.Fori(1, NG) as it:
                group(it, False)
            scan(NG - 1, GT - 1)
            add_skip(NG - 1, DT_ - 1)
            for k in range(B * CT):
                dve.wait_ge(S["op_ps"], k + 1)
                dve.tensor_scalar(XG[:, k // CT, k % CT], pair(k), CLAMP, -CLAMP, ALU.min, ALU.max).then_inc(S["op_rd"], 1)
            pixel_norm(1)
            dve.wait_ge(S["x1_rd"], B * CT)
            group_norm(1, XG2)
            dve.wait_ge(S["bn_ln"], 2)
            dve.tensor_tensor(INV[:, :], INV[:, :], BNG, ALU.mult).then_inc(S["bn_self"], 1)
            dve.wait_ge(S["bn_self"], 1)
            dve.tensor_tensor(SHF[:, :], BNM, INV[:, :], ALU.mult).then_inc(S["bn_self"], 1)
            dve.wait_ge(S["bn_self"], 2)
            dve.tensor_tensor(SHF[:, :], BNB, SHF[:, :], ALU.subtract).then_inc(S["bn_rd"], 1)
            dve.wait_ge(S["bn_rd"], 1)

            def take_states(b):
                for w in range(4):
                    i = 4 * b + w
                    dve.wait_ge(S["vk_ps"], i + 1)
                    if b:
                        dve.wait_ge(S["nd_ps"], 16 * b)
                    dve.tensor_copy(KS[:, w:w + 1], bank(3, w % 2)[:, P:P + 1]).then_inc(S["ks_rd"], 1)
                    dve.tensor_tensor(VKS[w][:, 0, :], bank(3, w % 2)[:, 0:P], MASK, ALU.mult).then_inc(S["vks_rd"], 1)
                    dve.wait_ge(S["ks_rd"], i + 1)
                    dve.tensor_scalar(VKS[w][:, 1, :], MASK, KS[:, w:w + 1], None, ALU.mult).then_inc(S["vks_rd"], 1)

            def divide(u):
                b, i = divmod(u, 8)
                w, c = divmod(i, 2)
                dve.wait_ge(S["nd_ps"], 2 * u + 2)
                dve.wait_ge(S["den_rd"], u + 1)
                dve.tensor_tensor(QR[b][:, w, c * HALF:(c + 1) * HALF], bank(attend_pair(u), 0), den_slot(u), ALU.mult).then_inc(S["o_rd"], 1)

            def add_projected(p):
                b, i = divmod(p, 4)
                m, c = divmod(i, 2)
                half = X[:, b, m, c * HALF:(c + 1) * HALF]
                dve.wait_ge(S["pr_ps"], p + 1)
                dve.scalar_tensor_tensor(out=half, in0=bank(2 - m * b, c), scalar=INV[:, m:m + 1], in1=half, op0=ALU.mult, op1=ALU.add).then_inc(S["pr_rd"], 1)

            def dve_between(n, c):
                for what, i in between(n, c):
                    if what == "states":
                        take_states(i)
                    elif what == "attend":
                        divide(i)
                    elif what == "project":
                        add_projected(i)

            for n in range(B * QT):
                b, j = divmod(n, QT)
                t = ORDER[j]
                dve.wait_ge(S["pad_rd"], n + 1)
                for i in range(DV_TAPS):
                    k = PE_TAPS + POOL_TAPS + i
                    partial = pair(1).rearrange("p (y x) -> p y x", x=HW)
                    if i == 0:
                        dve.wait_ge(S["pool_add"], (POOL_TAPS - 1) * (n + 1))
                        if n:
                            dve.wait_ge(S["acc_rd"], n)
                    else:
                        dve.wait_ge(S["acc_self"], (DV_TAPS - 1) * n + i)
                    if i == DV_TAPS - 1 and n >= 2:
                        dve.wait_ge(S["cv_ps"], 2 * n - 2)
                    ins = dve.scalar_tensor_tensor(out=ACC[:, n % 2] if i == DV_TAPS - 1 else partial, in0=tap(b, t, k), scalar=DW[:, t, k:k + 1],
                                                   in1=partial if i else PSUMS[n % 2], op0=ALU.mult, op1=ALU.add)
                    ins.then_inc(S["acc_rd"] if i == DV_TAPS - 1 else S["acc_self"], 1)
                    if n and i in (DV_TAPS // 3, DV_TAPS - 2):
                        dve_between(n - 1, 0 if i == DV_TAPS // 3 else 1)
                    if n < B * CT and i == 3:
                        k = divmod(n, CT)
                        dve.tensor_scalar(X[:, k[0], k[1]], X[:, k[0], k[1]], SHF[:, k[1]:k[1] + 1], None, ALU.add).then_inc(S["bn_rd"], 1)
            dve.wait_ge(S["bn_rd"], 1 + B * CT)
            for c in range(2):
                dve_between(B * QT - 1, c)


def constants():
    import numpy as np
    p = np.arange(P)
    same_head = (p[:, None] // HD == p[None, :] // HD).astype(np.float32)
    cst = np.zeros((P, 6, P), np.float32)
    cst[:, 0] = same_head / HD
    cst[:, 1] = 1.0 / C
    cst[:, 2] = np.eye(P, dtype=np.float32)
    for n in range(NS):
        cst[R + n, 3, n::NS] = 1.0
        cst[R + NS + n, 4, n::NS] = 1.0
    cst[:, 5] = same_head
    selr = np.zeros((P, 4, 32), np.float32)
    selb = np.zeros((P, 4, P), np.float32)
    for j in range(4):
        for d in range(OCT):
            selr[d * NS:(d + 1) * NS, j, OCT * j + d] = 1.0
            for i in range(PARTS + 1):
                selb[32 * i + OCT * j + d, j, d * NS:(d + 1) * NS] = 1.0
    return cst, selr, selb


def kernel(**inputs):
    import numpy as _np
    import concourse.bacc as _bacc
    from concourse import mybir as _mybir
    from concourse.bass_utils import run_bass_kernel_spmd as _run

    v = {n.replace("L0_conv_", "a_").replace("L1_conv_", "b_"): _np.asarray(t) for n, t in inputs.items()}
    by_tile = lambda t: t.reshape(-1, P).T
    by_role = lambda t: t.reshape(C // HD, 3, HD, -1).swapaxes(0, 1).reshape(QC, -1)
    cst, selr, selb = constants()
    cols = _np.concatenate([
        by_tile(v["a_norm_w"]), by_tile(v["a_norm_b"]),
        v["a_conv_w"].reshape(DT_, P, KC).swapaxes(0, 1).reshape(P, DT_ * KC),
        by_tile(v["a_conv_b"]), by_tile(v["a_dt_proj_b"]), by_tile(v["a_D"]),
        by_tile(v["b_bn_gamma"]), by_tile(v["b_bn_beta"]), by_tile(v["b_bn_mean"]), by_tile(v["b_bn_var"])], axis=1)
    laid = {
        "x": v["x"].reshape(B, C, L),
        "win": v["a_in_proj_w"].T, "xpw": v["a_x_proj_w"].T, "dtw": v["a_dt_proj_w"].T,
        "alogr": v["a_A_log"], "alog": v["a_A_log"].reshape(DI // OCT, P).T, "wout": v["a_out_proj_w"].T,
        "wq": by_role(v["b_qkv_w"]).T, "wpr": v["b_proj_w"].T,
        "dw": by_role(v["b_dw_w"]),
        "pw": v["b_pw_w"].reshape(C // HD, 3, HD, HD).transpose(1, 0, 3, 2).reshape(QC, HD),
        "cols": cols, "cst": cst, "selr": selr, "selb": selb.astype(_mybir.dt.np(BF16)),
    }
    nc = _bacc.Bacc("TRN2", target_bir_lowering=False, num_devices=1)
    arrays, args = {}, {}
    for name, t in laid.items():
        t = _np.ascontiguousarray(t)
        arrays[f"in_{name}"] = t
        args[name] = nc.dram_tensor(f"in_{name}", t.shape, _mybir.dt.from_np(t.dtype), kind="ExternalInput").ap()
    out = nc.dram_tensor("out_0", (B, C, L), F32, kind="ExternalOutput").ap()
    mamba_attention_kernel(nc, args, out)
    r = _run(nc, [arrays], core_ids=[0])
    return r.results[0]["out_0"].reshape(B, C, HW, HW)
```

```python
from contextlib import ExitStack

import concourse.bass as bass
from concourse import mybir

ALU = mybir.AluOpType
ACT = mybir.ActivationFunctionType
F32 = mybir.dt.float32
BF16 = mybir.dt.bfloat16

P = 128
B = 2
C = 256
CT = C // P
HW = 32
L = HW * HW
HALF = 512
DI = 512
DT_ = DI // P
NS = 16
R = 16
XD = R + 2 * NS
KC = 4
OCT = P // NS
GT = P // OCT
NG = B * DT_
PARTS = 3
QC = 3 * C
QT = QC // P
HD = 8
PAD = 2
PW = HW + 2 * PAD
TAPS = 25
PE_TAPS = (6,) * 11 + (3,)
POOL_TAPS = (3, 5) + (6,) * 9 + (7,)
BLK = L // P
ORDER = (2, 3, 4, 5, 0, 1)
CAP = 2.0
LOG_A_CAP = 20.0
CLAMP = 10.0
LN_EXP = "natural_log_exp_and_others"
EPS = 1e-5
EPS_ATT = 1e-15


def mamba_attention_kernel(nc, a, out):
    with ExitStack() as ctx:
        def sb(name, shape, dt=F32):
            return ctx.enter_context(nc.sbuf_tensor(name, shape, dt))

        def sem(name):
            return ctx.enter_context(nc.semaphore(name))

        X = sb("X", [P, B, CT, L])[:, :, :, :]
        arena = sb("arena", [P, 20480])
        mid = sb("mid", [P, 20480])

        def view(t, at, *shape):
            n = 1
            for s in shape:
                n *= s
            names = "abcd"[:len(shape)]
            pat = f"p ({' '.join(names)}) -> p {' '.join(names)}"
            return t[:, at:at + n].rearrange(pat, **dict(zip(names, shape)))

        XG = view(arena, 0, B, CT, L)
        SQ = view(arena, 4096, B, CT, L)
        RS = view(arena, 14336, B, L)
        XIN = view(arena, 8192, 2, L + KC - 1)
        CA = view(arena, 16384, 2, L)
        XDB = view(arena, 12288, B, L)
        DTF = view(arena, 0, 2, L)
        DXF = view(arena, 2048, 2, L)
        DTR, DXR = arena[:, 4096:5120], arena[:, 5120:6144]
        dt_parts = arena[:, 6144:10240].bitcast(BF16).rearrange("p (r i l) -> p r i l", r=2, i=PARTS + 1)
        HT = arena[:, 10240:11264].bitcast(BF16).rearrange("p (r l) -> p r l", r=2)
        VV = (arena[:, 11264:12288], arena[:, 19456:20480])
        dx_parts = arena[:, 16384:19456].bitcast(BF16).rearrange("p (r i l) -> p r i l", r=2, i=PARTS)

        def high(t):
            return t.bitcast(BF16).rearrange("p (l h) -> p l h", h=2)[:, :, 1]

        H = view(arena, 0, 4, L)
        G = view(arena, 4096, 8, L)
        stack = arena[:, 12288:20480].bitcast(BF16).rearrange("p (s k q l) -> p s k q l", s=2, k=2, q=4)
        XC = view(mid, 0, NG, L)
        SZ = view(mid, 8192, NG, L)
        BR = view(mid, 16384, B, L)
        CR = view(mid, 18432, B, L)
        PADB = arena[:, 0:B * QT * PW * PW].rearrange("p (b t y x) -> p b t y x", b=B, t=QT, y=PW)
        WT = view(arena, 15552, 2, max(PE_TAPS), P)
        ACC = view(arena, 18432, 2, HW, HW)
        SUM1 = view(arena, 17408, HW, HW)
        XO = view(mid, 8192, B, CT, L)
        SQO = view(mid, 12288, B, CT, L)
        RSO = (mid[:, 18464:19488], mid[:, 16416:17440])
        XG2 = view(mid, 0, B, CT, L)
        QR = (view(mid, 4096, 4, L), view(mid, 0, 4, L))
        KT = view(mid, 8192, BLK, 4, P)
        VT = view(mid, 12288, BLK, 4, P + 1)
        TMP = view(mid, 16416, 2, L)
        PROD = view(mid, 18464, HW, HW)
        DEN0 = mid[:, 19488:19488 + HALF]

        WIN = sb("WIN", [P, CT, 2 * DI])[:, :, :]
        LNB = WIN[:, :, :]
        win_flat = WIN.rearrange("p t n -> p (t n)")
        WQ = win_flat[:, 0:CT * QC].rearrange("p (t n) -> p t n", t=CT)
        win_rest = win_flat[:, CT * QC:]
        DIAG = win_rest[:, 0:P]
        WOUT = sb("WOUT", [P, DT_, C])[:, :, :]
        WPR = sb("WPR", [P, 4, C])[:, :, :]
        UM1 = WPR.rearrange("p t c -> p (t c)")
        XPW = sb("XPW", [P, DT_, XD])
        SUM0 = WOUT.rearrange("p t c -> p (t c)").rearrange("p (y x) -> p y x", x=HW)
        POOL_SUMS = (SUM0, SUM1)
        DTW = sb("DTW", [P, DI])
        VKS = [t.rearrange("p (i c) -> p i c", c=P) for t in (win_rest[:, 0:2 * P], win_rest[:, 2 * P:], DTW[:, 0:2 * P], DTW[:, 2 * P:])]
        cst = sb("cst", [P, 6, P])
        GRP8, ONES, IDENT, REPB, REPC, MASK = (cst[:, i, :] for i in range(6))
        SELR = sb("SELR", [P, 4, 32])
        SELB = arena[:, 10256:10512].bitcast(BF16).rearrange("p (j n) -> p j n", j=4)
        SELX = X.rearrange("p b t l -> p (b t l)").bitcast(BF16).rearrange("p (g q j n) -> p g q j n", g=DT_, q=4, j=4)
        ALR = SZ[96:P].rearrange("p e l -> p (e l)").rearrange("p (o j n) -> p o j n", o=DT_ * 4, j=4)
        AC = sb("AC", [P, DI // OCT])
        COLS = sb("COLS", [P, 40])
        NW, NB = COLS[:, 0:2], COLS[:, 2:4]
        CW = COLS[:, 4:20].rearrange("p (t k) -> p t k", k=KC)
        CB, DTB, DD = COLS[:, 20:24], COLS[:, 24:28], COLS[:, 28:32]
        BNG, BNB, BNM, BNV = (COLS[:, 32 + 2 * i:34 + 2 * i] for i in range(4))
        DW = sb("DW", [P, QT, TAPS])
        PWN = sb("PWN", [P, QT, HD])
        PWB = sb("PWB", [P, QT, P])
        ST = sb("ST", [P, 4, 2, 6])
        MV = sb("MV", [P, 4, 2])
        GM = sb("GM", [P, 4])
        GV = sb("GV", [P, 4])
        GR = sb("GR", [P, 4])
        EPSC = sb("EPSC", [P, 1])
        EPSA = sb("EPSA", [P, 1])
        INV = sb("INV", [P, 2])
        SHF = sb("SHF", [P, 2])
        KS = sb("KS", [P, 4])
        APROD = sb("APROD", [P, HW, HW])
        PS = ctx.enter_context(nc.psum_tensor("PS", [P, 8, HALF], F32))

        def pair(k):
            return PS[:, 2 * k:2 * k + 2, :].rearrange("p a b -> p (a b)")

        def bank(k, c):
            return PS[:, 2 * k + c, :]

        GN_PAIR = ((1, 3), (1, 1))
        MEAN_PAIR = ((2, 0), (2, 2))
        VAR_PAIR = ((1, 3), (1, 3))
        OP_PAIR = ((0, 1), (3, 0))

        def den_slot(u):
            return DEN0 if u < 8 else TMP[:, u % 2, 0:HALF]

        def project_pair(p):
            return 2 if p < 4 else (3, 0)[(p - 4) // 2]

        def attend_pair(u):
            return 1 if u >= 8 and u % 2 else 2

        def tap(b, t, k, c=None):
            dy, dx = divmod(k, 5)
            y, rows = (dy, HW) if c is None else (dy + HW // 2 * c, HW // 2)
            return PADB[:, b, t, y:y + rows, dx:dx + HW]

        dt_scratch = nc.dram_tensor("dt_parts", (NG, PARTS + 1, P, L), BF16, kind="Internal").ap()
        dx_scratch = nc.dram_tensor("dx_parts", (NG, PARTS, P, L), BF16, kind="Internal").ap()

        names = """ld_x_b0 ld_x_b1 ld_cst ld_c ld_w0 ld_w1 eps_set pad_set
            gn_bn gn_stat gn_mid gn_pre gn_mu_ps gn_dev gn_v gn_var_ps gn_ln gn_rstd gn_out
            ln_mu_ps ln_cent ln_sq ln_var_ps ln_lnv ln_rstd ln_self ln_out
            ip_ps xin_rd conv_self conv_out xc_rd sz_rd
            xd_zero xd_ps xd_rd rep_ps brep_rd crep_rd
            dt_ps sp_abs sp_exp sp_ln um1_rd sp_corr sp_sum v_rd dt_rd dx_rd hi_rd dt_r dx_r mid_rd dt_lo dx_lo dxhi_rd dxmid_rd alr_le
            dt_st0 dt_st1 dx_st0 dx_st1 ld_sel ld_alr ld_x1 selx_rd ex_lim ex_rd hic_rd stk_zero0 stk_zero1 stk_ld0 stk_ld1 a_exp a_rd
            bc_dt bc_dx da_rd u_rd scan_rd g_rd red_ps diag_rd y_rd
            op_ps op_rd x1_rd
            pwb_rd pad_zero bn_ln bn_self bn_rd qkv_ps pad_rd q_rd tr_ps kv_rd one_set
            wt_rd pool_first pool_prod act_prod pool_add acc_self acc_rd cv_ps cv_rd tmp_rd vk_ps ks_rd vks_rd nd_ps den_ln den_rd o_rd pr_ps pr_rd st_out""".split()
        S = {n: sem(n) for n in names}
        dt_st = [S[f"dt_st{r}"] for r in range(2)]
        dx_st = [S[f"dx_st{r}"] for r in range(2)]
        stk_ld = [S["stk_ld0"], S["stk_ld1"]]

        block = ctx.enter_context(nc.Block())

        def dve_taps(n):
            return TAPS - PE_TAPS[n] - POOL_TAPS[n]

        def by_scalar(n):
            return (2, 4) if n >= 3 else ()

        def pool_adds(n):
            return sum(POOL_TAPS[k] - 1 for k in range(n))

        def pool_products(n):
            return sum(POOL_TAPS[k] - 1 - len(by_scalar(k)) for k in range(n))

        def scalar_products(n):
            return sum(len(by_scalar(k)) for k in range(n))

        def dve_partials(n):
            return sum(dve_taps(k) - 1 for k in range(n))

        FROM_XD = (("dt", 0), ("dt", 1), ("dt", 2), ("b", 0), ("c", 0), ("dt", 3), ("b", 1), ("c", 1), ("dt", 4), ("dt", 5), ("dt", 6), ("dt", 7))

        def from_xd_pair(what, i):
            return (2 + FROM_XD.index((what, i))) % 4

        def between(n, c):
            steps = {(1, 0): [("to_pixels", 4)], (2, 0): [("to_pixels", 5)], (3, 0): [("to_pixels", 6)],
                     (4, 0): [("to_pixels", 7)], (4, 1): [("states", 0)],
                     (5, 0): [("to_pixels", 8), ("attend", 0)], (5, 1): [("to_pixels", 9), ("attend", 1), ("to_pixels", 10)],
                     (6, 0): [("to_pixels", 11), ("attend", 2)], (6, 1): [("attend", 3)],
                     (7, 0): [("attend", 4)], (7, 1): [("attend", 5), ("to_pixels", 12)],
                     (8, 0): [("attend", 6)], (8, 1): [("attend", 7), ("to_pixels", 13)],
                     (9, 0): [("project", 0)], (9, 1): [("project", 1), ("to_pixels", 14)],
                     (10, 0): [("project", 2), ("to_pixels", 15)], (10, 1): [("project", 3), ("states", 1)],
                     (11, 0): [("attend", 8), ("attend", 9)],
                     (11, 1): [("attend", 10), ("attend", 11), ("project_heads", 0), ("attend", 12), ("attend", 13), ("project_heads", 1),
                               ("attend", 14), ("attend", 15), ("project_heads", 2), ("project_heads", 3)] + [("project", p) for p in range(4, 8)]}
            return steps.get((n, c), [])

        @block.sync
        def _(sp):
            for b in range(B):
                sp.dma_start(X[:, b], a["x"][b].rearrange("(t p) l -> p t l", p=P)).then_inc(S[f"ld_x_b{b}"], 16)
            sp.wait_ge(S["ld_cst"], 16)
            sp.dma_start(ALR, a["alogr"].rearrange("(z c) n -> z (c n)", z=1).broadcast_to([32, DI * NS])
                         .rearrange("p (o j n) -> p o j n", o=DT_ * 4, j=4)).then_inc(S["ld_alr"], 16)
            sp.dma_start(WIN[:, :, :], a["win"].rearrange("(t p) n -> p t n", p=P)).then_inc(S["ld_w0"], 16)
            sp.dma_start(XPW[:, :, :], a["xpw"].rearrange("(t p) n -> p t n", p=P)).then_inc(S["ld_w0"], 16)
            sp.wait_ge(S["pad_set"], 2)
            sp.dma_start(DTW[0:R, :], a["dtw"]).then_inc(S["ld_w0"], 16)
            sp.dma_start(AC[:, :], a["alog"]).then_inc(S["ld_w0"], 16)
            sp.dma_start(WOUT[:, :, :], a["wout"].rearrange("(t p) n -> p t n", p=P)).then_inc(S["ld_w0"], 16)
            sp.dma_start(DW[:, :, :], a["dw"].rearrange("(t p) n -> p t n", p=P)).then_inc(S["ld_w0"], 16)
            sp.dma_start(PWN[:, :, :], a["pw"].rearrange("(t p) n -> p t n", p=P)).then_inc(S["ld_w0"], 16)
            sp.wait_ge(S["gn_out"], 4)
            for o in range(DT_ * 4):
                sp.dma_start(SELX[0:96, o // 4, o % 4], a["selb"][0:96]).then_inc(S["ld_sel"], 16)

            def load_stack(e, s):
                for k, scratch in enumerate((dt_scratch, dx_scratch)):
                    for i in range(PARTS + 1 - k):
                        sp.dma_start(stack[32 * i:32 * i + 32, s, k],
                                     scratch[e, i].rearrange("(q c) l -> c q l", c=32)).then_inc(stk_ld[s], 16)

            for e in range(NG):
                for part in ("hic_rd", "mid_rd", "dt_lo"):
                    sp.wait_ge(S[part], e + 1)
                sp.dma_start(dt_scratch[e].rearrange("i p l -> p i l"), dt_parts[:, e % 2]).then_inc(dt_st[e % 2], 16)
                for part in ("dxhi_rd", "dxmid_rd", "dx_lo"):
                    sp.wait_ge(S[part], e + 1)
                sp.dma_start(dx_scratch[e].rearrange("i p l -> p i l"), dx_parts[:, e % 2]).then_inc(dx_st[e % 2], 16)
                if e == NG - 3:
                    sp.wait_ge(S["dt_ps"], NG)
                    sp.wait_ge(S["stk_zero0"], 1)
                    sp.wait_ge(dt_st[0], 16)
                    sp.wait_ge(dx_st[0], 16)
                    load_stack(0, 0)
            for r in range(2):
                sp.wait_ge(dt_st[r], 16 * NG // 2)
                sp.wait_ge(dx_st[r], 16 * NG // 2)
            sp.wait_ge(S["stk_zero1"], 1)
            load_stack(1, 1)
            with sp.Fori(1, NG // 2) as n:
                for s in range(2):
                    sp.wait_ge(S["bc_dt"], 16 * (2 * n + s) - 16)
                    load_stack(2 * n + s, s)
            sp.wait_ge(S["dt_rd"], NG)
            sp.dma_start(WQ, a["wq"].rearrange("(t p) n -> p t n", p=P)).then_inc(S["ld_w1"], 16)
            sp.dma_start(WPR, a["wpr"].rearrange("(t p) n -> p t n", p=P)).then_inc(S["ld_w1"], 16)
            sp.wait_ge(S["bc_dt"], GT * NG)
            for b in range(B):
                sp.dma_start(X[:, b], a["x"][b].rearrange("(t p) l -> p t l", p=P)).then_inc(S["ld_x1"], 16)
            for b in range(B):
                for m in range(CT):
                    sp.wait_ge(S["pr_rd"], 4 * b + 2 * m + 2)
                    sp.dma_start(out[b, m * P:(m + 1) * P, :], X[:, b, m]).then_inc(S["st_out"], 16)
            sp.wait_ge(S["st_out"], 16 * B * CT)

        @block.gpsimd
        def _(pool):
            pool.memset(EPSC[:, :], EPS).then_inc(S["eps_set"], 1)
            pool.memset(EPSA[:, :], EPS_ATT).then_inc(S["eps_set"], 1)
            pool.memset(XIN[:, :, 0:KC - 1], 0.0).then_inc(S["pad_set"], 1)
            pool.memset(DTW[:, :], 0.0).then_inc(S["pad_set"], 1)
            pool.memset(XDB[:, :, :], 0.0).then_inc(S["xd_zero"], 1)
            pool.wait_ge(S["eps_set"], 2)
            pool.wait_ge(S["pad_set"], 2)
            pool.wait_ge(S["xd_zero"], 1)
            pool.wait_ge(S["alr_le"], 1)
            pool.wait_ge(S["ld_cst"], 16)
            pool.wait_ge(S["ld_c"], 48)
            pool.wait_ge(S["gn_out"], 4)
            for j in range(4):
                pool.tensor_tensor(SELX[96:P].rearrange("p g q j n -> p (g q) j n")[:, :, j, :], ALR[:, :, j, :],
                                   SELB[96:P, j:j + 1, :].broadcast_to([32, DT_ * 4, P]), ALU.mult).then_inc(S["selx_rd"], 1)
            pool.wait_ge(S["ld_w0"], 112)
            pool.wait_ge(S["selx_rd"], 4)
            for t in range(QT):
                pool.tensor_tensor(PWB[:, t, :].rearrange("p (g o) -> p g o", o=HD),
                                   MASK.rearrange("p (g o) -> p g o", o=HD),
                                   PWN[:, t:t + 1, :].broadcast_to([P, P // HD, HD]), ALU.mult).then_inc(S["pwb_rd"], 1)
            pool.wait_ge(S["pwb_rd"], QT)
            pool.wait_ge(S["ln_out"], B * CT)
            pool.memset(stack[96:P, 0, 1], 0.0).then_inc(S["stk_zero0"], 1)
            pool.wait_ge(S["stk_zero0"], 1)
            for i in range(NG + 1):
                if i >= 1:
                    e = i - 1
                    if e >= 2:
                        pool.wait_ge(S["dxhi_rd"], e - 1)
                        pool.wait_ge(S["dx_r"], e - 1)
                    pool.wait_ge(S["dt_rd"], e + 1)
                    pool.tensor_tensor(DXF[:, e % 2], DTF[:, e % 2], XC[:, e], ALU.mult).then_inc(S["dx_rd"], 1)
                if i < NG:
                    pool.wait_ge(S["sp_ln"], i + 1)
                    pool.wait_ge(S["um1_rd"], i + 1)
                    pool.tensor_tensor(LNB[:, i % 2], LNB[:, i % 2], UM1[:, :], ALU.subtract).then_inc(S["sp_corr"], 1)
                if i >= 1:
                    if e >= 1:
                        pool.wait_ge(S["dxmid_rd"], e)
                        pool.wait_ge(S["dx_lo"], e)
                    pool.wait_ge(S["dx_rd"], e + 1)
                    pool.tensor_tensor(DXR, DXF[:, e % 2], high(DXF[:, e % 2]), ALU.subtract).then_inc(S["dx_r"], 1)
                    if e >= 2:
                        pool.wait_ge(dx_st[e % 2], 16 * (e // 2))
                    pool.wait_ge(S["dx_r"], e + 1)
                    pool.tensor_tensor(dx_parts[:, e % 2, 2], DXR, high(DXR), ALU.subtract).then_inc(S["dx_lo"], 1)
            for r in range(2):
                pool.wait_ge(dt_st[r], 16 * NG // 2)
                pool.wait_ge(dx_st[r], 16 * NG // 2)

            def mult_c(it, b, first):
                for t in range(GT):
                    pool.wait_ge(S["scan_rd"], GT * it + t + 1)
                    if not first or t >= 8:
                        pool.wait_ge(S["red_ps"], 4 * it + t // 4 - 1)
                    pool.tensor_tensor(G[:, t % 8], H[:, t % 4], CR[:, b], ALU.mult).then_inc(S["g_rd"], 1)

            pool.wait_ge(S["crep_rd"], B)
            mult_c(0, 0, True)
            for b in range(B):
                with pool.Fori(max(1, b * DT_), (b + 1) * DT_) as it:
                    mult_c(it, b, False)
            pool.wait_ge(S["red_ps"], 4 * NG)
            pool.wait_ge(S["bc_dt"], GT * NG)
            pool.wait_ge(S["g_rd"], GT * NG)
            images = PADB.rearrange("p b t y x -> p (b t) y x")
            for edge in (slice(0, PAD), slice(PAD + HW, PW)):
                pool.memset(images[:, :, edge, :], 0.0).then_inc(S["pad_zero"], 1)
                pool.memset(images[:, :, PAD:PAD + HW, edge], 0.0).then_inc(S["pad_zero"], 1)
            def tap_weights(n):
                if n >= 2:
                    pool.wait_ge(S["cv_ps"], 2 * n - 2)
                t = ORDER[n % QT]
                shape = [P, PE_TAPS[n], P]
                pool.tensor_tensor(WT[:, n % 2, 0:PE_TAPS[n]], PWB[:, t:t + 1, :].broadcast_to(shape),
                                   DW[:, t, 0:PE_TAPS[n]].unsqueeze(2).broadcast_to(shape), ALU.mult).then_inc(S["wt_rd"], 1)

            tap_weights(0)
            tap_weights(1)
            pool.wait_ge(S["x1_rd"], CT)
            for n in range(B * QT):
                b, t = n // QT, ORDER[n % QT]
                pool.wait_ge(S["pad_rd"], n + 1)
                if n >= 2:
                    pool.wait_ge(S["acc_self"], dve_partials(n - 2) + 1)
                own, others = pool_products(n), scalar_products(n)
                for i in range(POOL_TAPS[n]):
                    if n >= 3 and i == 3:
                        tap_weights(n - 1)
                    k = PE_TAPS[n] + i
                    win, w = tap(b, t, k), DW[:, t, k:k + 1]
                    if i == 0:
                        pool.tensor_scalar(POOL_SUMS[n % 2], win, w, 0.0, ALU.mult, ALU.add).then_inc(S["pool_first"], 1)
                        pool.wait_ge(S["pool_first"], n + 1)
                        continue
                    adds = pool_adds(n) + i - 1
                    if adds:
                        pool.wait_ge(S["pool_add"], adds)
                    if i in by_scalar(n):
                        others += 1
                        pool.wait_ge(S["act_prod"], others)
                        pool.tensor_tensor(POOL_SUMS[n % 2], POOL_SUMS[n % 2], APROD[:, :, :], ALU.add).then_inc(S["pool_add"], 1)
                    else:
                        own += 1
                        pool.tensor_scalar(PROD, win, w, 0.0, ALU.mult, ALU.add).then_inc(S["pool_prod"], 1)
                        pool.wait_ge(S["pool_prod"], own)
                        pool.tensor_tensor(POOL_SUMS[n % 2], POOL_SUMS[n % 2], PROD, ALU.add).then_inc(S["pool_add"], 1)
                if n == B * QT - 1:
                    tap_weights(n)

        @block.scalar
        def _(act):
            act.dma_start(cst[:, :, :], a["cst"]).then_inc(S["ld_cst"], 16)
            act.dma_start(SELR[:, :, :], a["selr"]).then_inc(S["ld_c"], 16)
            act.dma_start(SELB, a["selb"]).then_inc(S["ld_c"], 16)
            act.dma_start(COLS[:, :], a["cols"]).then_inc(S["ld_c"], 16)
            act.preload_act_table_set(LN_EXP)
            act.wait_ge(S["eps_set"], 2)

            def group_rstd(n):
                ph, b = divmod(n, B)
                cols = slice(CT * b, CT * b + CT)
                act.wait_ge(S["gn_var_ps"], n + 1)
                act.activation(GR[:, cols], bank(GN_PAIR[ph][b], 1)[:, 0:CT], ACT.Ln, bias=EPSC[:, :]).then_inc(S["gn_ln"], 1)
                act.wait_ge(S["gn_ln"], n + 1)
                act.activation(GR[:, cols], GR[:, cols], ACT.Exp, scale=-0.5).then_inc(S["gn_rstd"], 1)

            def squares(n):
                ph, b = divmod(n, B)
                for t in range(CT):
                    act.wait_ge(S["ln_cent"], CT * n + t + 1)
                    act.activation((SQ, SQO)[ph][:, b, t], (XG, XO)[ph][:, b, t], ACT.Square).then_inc(S["ln_sq"], 1)

            def pixel_rstd(n):
                ph, b = divmod(n, B)
                dst = RSO[b] if ph else RS[:, b]
                act.wait_ge(S["ln_var_ps"], n + 1)
                act.activation(dst, pair(VAR_PAIR[ph][b]), ACT.Ln, bias=EPSC[:, :]).then_inc(S["ln_lnv"], 1)
                act.wait_ge(S["ln_lnv"], n + 1)
                act.activation(dst, dst, ACT.Exp, scale=-0.5).then_inc(S["ln_rstd"], 1)

            for b in range(B):
                group_rstd(b)
            act.wait_ge(S["ld_w0"], 112)
            act.activation(AC[:, :], AC[:, :], ACT.Exp).then_inc(S["a_exp"], 1)
            for b in range(B):
                squares(b)
            for b in range(B):
                pixel_rstd(b)

            def silu_xc(e):
                act.wait_ge(S["conv_out"], e + 1)
                act.activation(XC[:, e], CA[:, e % 2], ACT.Silu, bias=CB[:, e % DT_:e % DT_ + 1]).then_inc(S["xc_rd"], 1)

            act.wait_ge(S["pad_set"], 2)
            for b in range(B):
                for m in range(2 * DT_):
                    k = 2 * DT_ * b + m
                    act.wait_ge(S["ip_ps"], k + 1)
                    if m < DT_:
                        e = DT_ * b + m
                        if e >= 2:
                            act.wait_ge(S["conv_out"], e - 1)
                            act.wait_ge(S["xc_rd"], e - 1)
                        act.activation(XIN[:, e % 2, KC - 1:KC - 1 + L], pair(k % 4), ACT.Copy).then_inc(S["xin_rd"], 1)
                        act.activation(CA[:, e % 2], pair(k % 4), ACT.Copy, scale=CW[:, m, KC - 1:KC]).then_inc(S["xin_rd"], 1)
                    else:
                        if k == DT_:
                            act.wait_ge(S["selx_rd"], 4)
                        act.activation(SZ[:, DT_ * b + m - DT_], pair(k % 4), ACT.Silu).then_inc(S["sz_rd"], 1)
                    if 1 <= m <= DT_:
                        silu_xc(DT_ * b + m - 1)
            for b in range(B):
                act.wait_ge(S["xd_ps"], b + 1)
                act.wait_ge(S["xd_zero"], 1)
                act.activation(XDB[0:XD, b], pair(b)[0:XD, :], ACT.Copy).then_inc(S["xd_rd"], 1)

            def dx_middle(e):
                act.wait_ge(S["dx_r"], e + 1)
                act.activation(dx_parts[:, e % 2, 1], high(DXR), ACT.Copy).then_inc(S["dxmid_rd"], 1)

            act.preload_act_table_set(LN_EXP)
            for i in range(NG + 1):
                if i < NG:
                    if i >= 2:
                        act.wait_ge(S["dx_rd"], i - 1)
                        act.wait_ge(S["dt_r"], i - 1)
                        act.wait_ge(S["hi_rd"], i - 1)
                    act.wait_ge(S["v_rd"], i + 1)
                    act.activation(DTF[:, i % 2], VV[i % 2], ACT.Abs).then_inc(S["sp_abs"], 1)
                    act.wait_ge(S["sp_abs"], i + 1)
                    act.activation(DTF[:, i % 2], DTF[:, i % 2], ACT.Exp, scale=-1.0).then_inc(S["sp_exp"], 1)
                    if i >= 2:
                        act.wait_ge(S["sp_sum"], i - 1)
                    act.wait_ge(S["sp_exp"], i + 1)
                    act.activation(LNB[:, i % 2], DTF[:, i % 2], ACT.Ln, bias=1.0).then_inc(S["sp_ln"], 1)
                if i >= 1:
                    e = i - 1
                    if e >= 2:
                        act.wait_ge(S["hic_rd"], e - 1)
                    if e >= 1:
                        dx_middle(e - 1)
                    act.wait_ge(S["dt_rd"], e + 1)
                    act.activation(HT[:, e % 2], high(DTF[:, e % 2]), ACT.Copy).then_inc(S["hi_rd"], 1)
                    if e >= 2:
                        act.wait_ge(dt_st[e % 2], 16 * (e // 2))
                        act.wait_ge(dx_st[e % 2], 16 * (e // 2))
                    act.wait_ge(S["dt_r"], e + 1)
                    act.activation(dt_parts[:, e % 2, 1], high(DTR), ACT.Copy).then_inc(S["mid_rd"], 1)
                    act.wait_ge(S["dx_rd"], e + 1)
                    act.activation(dx_parts[:, e % 2, 0], high(DXF[:, e % 2]), ACT.Copy).then_inc(S["dxhi_rd"], 1)
                if i in (0, 2):
                    b = i // 2
                    act.wait_ge(S["rep_ps"], 2 * b + 2)
                    act.activation(CR[:, b], pair(from_xd_pair("c", b)), ACT.Copy).then_inc(S["crep_rd"], 1)
            dx_middle(NG - 1)
            act.wait_ge(S["a_rd"], 1)
            act.wait_ge(S["sp_sum"], NG)

            def exp_group(it, g, first):
                for t in range(GT):
                    act.wait_ge(S["bc_dt"], GT * it + t + 1)
                    octave = GT * g + 4 * (t % 4) + t // 4
                    act.activation(pair(t % 2), pair(t % 2), ACT.Exp, scale=AC[:, bass.ds(octave, 1)]).then_inc(S["da_rd"], 1)
                    if t == 6:
                        if not first:
                            act.wait_ge(S["red_ps"], 4 * it)
                        act.activation(DIAG, IDENT, ACT.Copy, scale=DD[:, bass.ds(g, 1)]).then_inc(S["diag_rd"], 1)

            exp_group(0, 0, True)
            with act.Fori(1, NG) as it:
                exp_group(it, it & (DT_ - 1), False)
            act.preload_act_table_set("exp_and_others")
            squares(2)
            pixel_rstd(2)
            squares(3)
            group_rstd(2)
            pixel_rstd(3)
            act.activation(INV[:, :], BNV, ACT.Ln, bias=EPSC[:, :]).then_inc(S["bn_ln"], 1)
            act.wait_ge(S["bn_ln"], 1)
            act.activation(INV[:, :], INV[:, :], ACT.Exp, scale=-0.5).then_inc(S["bn_ln"], 1)

            def copy_kv_qkv(i):
                b, j = divmod(i, 8)
                act.wait_ge(S["pad_rd"], QT * b + j + 1)
                if i >= 2:
                    act.wait_ge(S["tr_ps"], i - 1)
                act.activation(TMP[:, i % 2].rearrange("p (y x) -> p y x", x=HW), PADB[:, b, 2 + j, PAD:PAD + HW, PAD:PAD + HW],
                               ACT.Copy).then_inc(S["tmp_rd"], 2)

            def evac_kv(i):
                b, w = divmod(i, 8)
                act.wait_ge(S["tr_ps"], i + 1)
                path, j = divmod(w, 4)
                src = pair(3).rearrange("p (k c) -> p k c", c=P)
                if w == 0 and b:
                    act.wait_ge(S["vk_ps"], 4 * b)
                if j < 2:
                    act.activation(KT[:, :, 2 * path + j, :], src, ACT.Relu).then_inc(S["kv_rd"], 1)
                else:
                    act.activation(VT[:, :, 2 * path + j - 2, 0:P], src, ACT.Copy).then_inc(S["kv_rd"], 1)

            def reciprocal(u):
                act.wait_ge(S["nd_ps"], 2 * u + 2)
                if 1 <= u < 8:
                    act.wait_ge(S["o_rd"], u)
                elif u >= 10:
                    act.wait_ge(S["o_rd"], u - 1)
                elif u >= 8:
                    act.wait_ge(S["tr_ps"], 8 * B)
                act.activation(den_slot(u), bank(attend_pair(u), 1), ACT.Ln, bias=EPSA[:, :]).then_inc(S["den_ln"], 1)
                act.wait_ge(S["den_ln"], u + 1)
                act.activation(den_slot(u), den_slot(u), ACT.Exp, scale=-1.0).then_inc(S["den_rd"], 1)

            def act_between(n, c):
                for what, i in between(n, c):
                    if what == "to_pixels":
                        evac_kv(i)
                        if i == 7:
                            copy_kv_qkv(8)
                            copy_kv_qkv(9)
                        elif i in (8, 9):
                            copy_kv_qkv(i + 2)
                    elif what == "attend":
                        reciprocal(i)

            act.wait_ge(S["pad_zero"], 4)
            for k in range(B * QT):
                b, j = divmod(k, QT)
                act.wait_ge(S["qkv_ps"], k + 1)
                act.activation(PADB[:, b, ORDER[j], PAD:PAD + HW, PAD:PAD + HW],
                               pair(k % 2 * 2).rearrange("p (y x) -> p y x", x=HW), ACT.Copy).then_inc(S["pad_rd"], 1)
                if k == 2:
                    group_rstd(3)
                    act.preload_act_table_set(LN_EXP)
                if k == 1:
                    act.wait_ge(S["one_set"], 1)
                if k in (1, 2, 3):
                    copy_kv_qkv(k - 1)
                    if k >= 2:
                        evac_kv(k - 2)
                elif k == 4:
                    copy_kv_qkv(3)
                    evac_kv(2)
                elif k == 5:
                    evac_kv(3)
            act.wait_ge(S["pad_rd"], B * QT)
            for b in range(B):
                for t in range(2):
                    act.activation(QR[b][:, t].rearrange("p (y x) -> p y x", x=HW), PADB[:, b, t, PAD:PAD + HW, PAD:PAD + HW],
                                   ACT.Relu).then_inc(S["q_rd"], 1)
            def product(n, i):
                b, t, k = n // QT, ORDER[n % QT], PE_TAPS[n] + i
                done = scalar_products(n) + by_scalar(n).index(i)
                if done:
                    m = n if i == by_scalar(n)[1] else n - 1
                    last = by_scalar(n)[0] if m == n else by_scalar(m)[1]
                    act.wait_ge(S["pool_add"], pool_adds(m) + last)
                act.activation(APROD[:, :, :], tap(b, t, k), ACT.Copy, scale=DW[:, t, k:k + 1]).then_inc(S["act_prod"], 1)

            for n in range(B * QT):
                b, j = divmod(n, QT)
                for c in range(2):
                    if n + 2 < B * QT:
                        for i in by_scalar(n + 2)[c:c + 1]:
                            product(n + 2, i)
                    act.wait_ge(S["cv_ps"], 2 * n + c + 1)
                    half = slice(c * HALF, (c + 1) * HALF)
                    if j < 4:
                        i = 8 * b + 4 + j
                        act.wait_ge(S["tr_ps"], i - 1)
                        act.activation(TMP[:, i % 2, half], bank(0, c), ACT.Copy).then_inc(S["tmp_rd"], 1)
                    else:
                        act.activation(QR[b][:, 2 + ORDER[j], half], bank(0, c), ACT.Relu).then_inc(S["cv_rd"], 1)
                    act_between(n, c)

        @block.tensor
        def _(pe):
            pe.wait_ge(S["ld_cst"], 16)

            def group_mean(n):
                ph, b = divmod(n, B)
                pe.wait_ge(S["gn_stat"], CT * (n + 1))
                pe.matmul(bank(GN_PAIR[ph][b], 0)[:, 0:CT], GRP8, MV[:, CT * b:CT * b + CT, 0], start=True, stop=True).then_inc(S["gn_mu_ps"], 1)

            def group_var(n):
                ph, b = divmod(n, B)
                pe.wait_ge(S["gn_v"], n + 1)
                pe.matmul(bank(GN_PAIR[ph][b], 1)[:, 0:CT], GRP8, GV[:, CT * b:CT * b + CT], start=True, stop=True).then_inc(S["gn_var_ps"], 1)

            def pixel_mean(n, ready, count):
                ph, b = divmod(n, B)
                pe.wait_ge(ready, count)
                for c in range(2):
                    for t in range(CT):
                        mm = pe.matmul(bank(MEAN_PAIR[ph][b], c), ONES, (XG, XO)[ph][:, b, t, c * HALF:(c + 1) * HALF], start=(t == 0), stop=(t == CT - 1))
                mm.then_inc(S["ln_mu_ps"], 1)

            def pixel_var(n):
                ph, b = divmod(n, B)
                pe.wait_ge(S["ln_sq"], CT * (n + 1))
                for c in range(2):
                    for t in range(CT):
                        mm = pe.matmul(bank(VAR_PAIR[ph][b], c), ONES, (SQ, SQO)[ph][:, b, t, c * HALF:(c + 1) * HALF], start=(t == 0), stop=(t == CT - 1))
                mm.then_inc(S["ln_var_ps"], 1)

            for b in range(B):
                group_mean(b)
            for b in range(B):
                group_var(b)
            for b in range(B):
                pixel_mean(b, S["gn_out"], CT * (b + 1))
            for b in range(B):
                pe.wait_ge(S["gn_rstd"], b + 1)
                pixel_var(b)
            pe.wait_ge(S["ld_w0"], 112)
            for b in range(B):
                pe.wait_ge(S["ln_out"], CT * (b + 1))
                for m in range(2 * DT_):
                    k = 2 * DT_ * b + m
                    if k < 4:
                        if k % 2 == 0:
                            pe.wait_ge(S["ln_cent"], CT * B)
                        else:
                            pe.wait_ge(S["ln_lnv"], (k + 1) // 2)
                    else:
                        kb, km = divmod(k - 4, 2 * DT_)
                        if km < DT_:
                            pe.wait_ge(S["xin_rd"], 2 * (DT_ * kb + km + 1))
                        else:
                            pe.wait_ge(S["sz_rd"], DT_ * kb + km - DT_ + 1)
                    for c in range(2):
                        for t in range(CT):
                            mm = pe.matmul(bank(k % 4, c), WIN[:, t, m * P:(m + 1) * P], XG[:, b, t, c * HALF:(c + 1) * HALF], start=(t == 0), stop=(t == CT - 1))
                    mm.then_inc(S["ip_ps"], 1)
            for b in range(B):
                pe.wait_ge(S["sz_rd"], DT_ + b + 1)
                pe.wait_ge(S["xc_rd"], DT_ * (b + 1))
                for c in range(2):
                    for t in range(DT_):
                        mm = pe.matmul(bank(b, c)[0:XD, :], XPW[:, t, :], XC[:, DT_ * b + t, c * HALF:(c + 1) * HALF], start=(t == 0), stop=(t == DT_ - 1))
                mm.then_inc(S["xd_ps"], 1)
            pe.wait_ge(S["pad_set"], 2)
            pe.wait_ge(S["sz_rd"], NG)
            pe.wait_ge(S["xd_rd"], B)
            taken = {"dt": "v_rd", "b": "brep_rd", "c": "crep_rd"}
            for j, (what, i) in enumerate(FROM_XD):
                if j >= 4:
                    before, k = FROM_XD[j - 4]
                    pe.wait_ge(S[taken[before]], k + 1)
                weights = DTW[:, (i % DT_) * P:(i % DT_ + 1) * P] if what == "dt" else {"b": REPB, "c": REPC}[what]
                b = i // DT_ if what == "dt" else i
                for c in range(2):
                    mm = pe.matmul(bank((2 + j) % 4, c), weights, XDB[:, b, c * HALF:(c + 1) * HALF], start=True, stop=True)
                mm.then_inc(S["dt_ps"] if what == "dt" else S["rep_ps"], 1)
            pe.wait_ge(S["brep_rd"], B)
            pe.wait_ge(S["crep_rd"], B)
            pe.wait_ge(S["v_rd"], NG)

            def spread(it, g, s, t, first):
                if t == 0:
                    pe.wait_ge(stk_ld[s], 112 * ((it >> 1) + 1))
                if not first or t >= 1:
                    pe.wait_ge(S["u_rd"], GT * it + t)
                for c in range(2):
                    mm = pe.matmul(bank(2, c), SELX[:, g, t % 4, t // 4, :], stack[:, s, 1, t % 4, c * HALF:(c + 1) * HALF], start=True, stop=True)
                mm.then_inc(S["bc_dx"], 1)
                if not first or t >= 2:
                    pe.wait_ge(S["scan_rd"], GT * it + t - 1)
                for c in range(2):
                    mm = pe.matmul(bank(t % 2, c), SELX[:, g, t % 4, t // 4, :], stack[:, s, 0, t % 4, c * HALF:(c + 1) * HALF], start=True, stop=True)
                mm.then_inc(S["bc_dt"], 1)

            def state_sum(it, k, c, quarters, first):
                if c == 0:
                    pe.wait_ge(S["g_rd"], GT * it + 4 * k + quarters[-1] + 1)
                if k == 0 and c == 0 and not first:
                    pe.wait_ge(S["y_rd"], it)
                for q in quarters:
                    mm = pe.matmul(bank(3, c)[32 * q:32 * q + 32, :], SELR[:, k, :], G[:, (4 * k + q) % 8, c * HALF:(c + 1) * HALF],
                                   start=(k == 0), stop=(k == 3))
                if c and quarters[-1] == 3:
                    mm.then_inc(S["red_ps"], 1)

            def skip(it, c):
                if c == 0:
                    pe.wait_ge(S["diag_rd"], it + 1)
                pe.matmul(bank(3, c), DIAG, XC[:, it, c * HALF:(c + 1) * HALF], start=False, stop=False)

            def group(it, s, first):
                g = 0 if first else it & (DT_ - 1)
                for t in range(GT):
                    spread(it, g, s, t, first)
                    if t in (7, 8):
                        state_sum(it, 0, t - 7, (0, 1, 2, 3), first)
                    elif t >= 9:
                        k, i = divmod(t - 5, 4)
                        state_sum(it, k, i % 2, ((0, 1), (2, 3))[i // 2], first)
                    elif t <= 4 and not first:
                        k, i = divmod(GT + t - 5, 4)
                        state_sum(it - 1, k, i % 2, ((0, 1), (2, 3))[i // 2], False)
                    if t in (11, 12):
                        skip(it, t - 11)

            pe.wait_ge(S["ld_c"], 48)
            pe.wait_ge(S["ld_sel"], 16 * DT_ * 4)
            pe.wait_ge(S["selx_rd"], 4)
            group(0, 0, True)
            with pe.Fori(0, NG // 2 - 1) as n:
                group(2 * n + 1, 1, False)
                group(2 * n + 2, 0, False)
            group(NG - 1, 1, False)
            for t in range(5):
                k, i = divmod(GT + t - 5, 4)
                state_sum(NG - 1, k, i % 2, ((0, 1), (2, 3))[i // 2], False)
            def out_proj(b, m):
                pe.wait_ge(S["y_rd"], DT_ * (b + 1))
                for c in range(2):
                    for t in range(DT_):
                        mm = pe.matmul(bank(OP_PAIR[b][m], c), WOUT[:, t, m * P:(m + 1) * P], XC[:, DT_ * b + t, c * HALF:(c + 1) * HALF], start=(t == 0), stop=(t == DT_ - 1))
                mm.then_inc(S["op_ps"], 1)

            pe.wait_ge(S["scan_rd"], GT * NG)
            pe.wait_ge(S["u_rd"], GT * NG)
            out_proj(0, 0)
            out_proj(0, 1)
            pixel_mean(2, S["op_rd"], 2)
            out_proj(1, 0)
            pixel_var(2)
            out_proj(1, 1)
            pe.wait_ge(S["ln_cent"], 3 * CT)
            pixel_mean(3, S["op_rd"], 4)
            pe.wait_ge(S["ln_lnv"], 3)
            group_mean(2)
            group_var(2)
            pixel_var(3)
            pe.wait_ge(S["ln_cent"], 4 * CT)
            pe.wait_ge(S["ld_w1"], 32)

            def to_pixels(i):
                pe.wait_ge(S["tmp_rd"], 2 * i + 2)
                if i >= 1:
                    pe.wait_ge(S["kv_rd"], i)
                if i == 8:
                    pe.wait_ge(S["vks_rd"], 8)
                    pe.wait_ge(S["ks_rd"], 4)
                for j in range(BLK):
                    mm = pe.transpose(bank(3, j // 4)[:, (j % 4) * P:(j % 4 + 1) * P], TMP[:, i % 2, j * P:(j + 1) * P], IDENT)
                mm.then_inc(S["tr_ps"], 1)

            def states(b):
                pe.wait_ge(S["kv_rd"], 8 * (b + 1))
                for w in range(4):
                    if w >= 2:
                        pe.wait_ge(S["vks_rd"], 8 * b + 2 * w - 2)
                        pe.wait_ge(S["ks_rd"], 4 * b + w - 1)
                    for j in range(BLK):
                        mm = pe.matmul(bank(3, w % 2)[:, 0:P + 1], KT[:, j, w, :], VT[:, j, w, :], start=(j == 0), stop=(j == BLK - 1))
                    mm.then_inc(S["vk_ps"], 1)

            def attend(u):
                b, i = divmod(u, 8)
                w, c = divmod(i, 2)
                pe.wait_ge(S["vks_rd"], 8 * b + 2 * w + 2)
                if w < 2:
                    pe.wait_ge(S["q_rd"], 2 * b + w + 1)
                else:
                    pe.wait_ge(S["cv_rd"], 2 * (2 * b + w - 2) + c + 1)
                if i == 0 and b:
                    pe.wait_ge(S["pr_rd"], 4 * b)
                if 1 <= u < 8:
                    pe.wait_ge(S["o_rd"], u)
                elif u >= 10:
                    pe.wait_ge(S["o_rd"], u - 1)
                for k in range(2):
                    pe.matmul(bank(attend_pair(u), k), VKS[w][:, k, :], QR[b][:, w, c * HALF:(c + 1) * HALF], start=True, stop=True).then_inc(S["nd_ps"], 1)

            def project(p):
                b, i = divmod(p, 4)
                m, c = divmod(i, 2)
                if b:
                    return
                if i == 0:
                    pe.wait_ge(S["o_rd"], 8)
                if i >= 2:
                    pe.wait_ge(S["pr_rd"], p - 1)
                for w in range(4):
                    mm = pe.matmul(bank(project_pair(p), c), WPR[:, w, m * P:(m + 1) * P], QR[b][:, w, c * HALF:(c + 1) * HALF], start=(w == 0), stop=(w == 3))
                mm.then_inc(S["pr_ps"], 1)

            def project_heads(w):
                if w == 0:
                    pe.wait_ge(S["kv_rd"], 8 * B)
                    pe.wait_ge(S["vks_rd"], 8 * B)
                    pe.wait_ge(S["cv_rd"], 4 * B)
                pe.wait_ge(S["o_rd"], 8 + 2 * w + 2)
                for p in range(4, 8):
                    m, c = divmod(p - 4, 2)
                    mm = pe.matmul(bank(project_pair(p), c), WPR[:, w, m * P:(m + 1) * P], QR[1][:, w, c * HALF:(c + 1) * HALF], start=(w == 0), stop=(w == 3))
                    if w == 3:
                        mm.then_inc(S["pr_ps"], 1)

            pe_steps = {"to_pixels": to_pixels, "states": states, "attend": attend, "project": project, "project_heads": project_heads}
            for k in range(B * QT):
                b, j = divmod(k, QT)
                t = ORDER[j]
                if j == 0:
                    pe.wait_ge(S["gn_out"], 4 + CT * (b + 1))
                if k >= 2:
                    pe.wait_ge(S["pad_rd"], k - 1)
                for c in range(2):
                    for u in range(CT):
                        mm = pe.matmul(bank(k % 2 * 2, c), WQ[:, u, t * P:(t + 1) * P], XG2[:, b, u, c * HALF:(c + 1) * HALF], start=(u == 0), stop=(u == CT - 1))
                mm.then_inc(S["qkv_ps"], 1)
                if k == 2:
                    pe.wait_ge(S["gn_rstd"], 3)
                    pe.wait_ge(S["ln_rstd"], 4)
                    group_mean(3)
                    group_var(3)
                if 2 <= k <= 5:
                    to_pixels(k - 2)
            pe.wait_ge(S["pad_rd"], B * QT)
            for n in range(B * QT):
                b, j = divmod(n, QT)
                t = ORDER[j]
                pe.wait_ge(S["wt_rd"], n + 1)
                for c in range(2):
                    if n:
                        pb, pj = divmod(n - 1, QT)
                        if pj < 4:
                            pe.wait_ge(S["tmp_rd"], 2 * (8 * pb + 4 + pj) + c + 1)
                        else:
                            pe.wait_ge(S["cv_rd"], 2 * (2 * pb + pj - 4) + c + 1)
                    for k in range(PE_TAPS[n]):
                        pe.matmul(bank(0, c), WT[:, n % 2, k, :], tap(b, t, k, c), start=(k == 0), stop=False)
                    pe.wait_ge(S["acc_rd"], n + 1)
                    pe.matmul(bank(0, c), PWB[:, t, :], ACC[:, n % 2, 16 * c:16 * c + 16, :], start=False, stop=True).then_inc(S["cv_ps"], 1)
                    for what, i in between(n, c):
                        pe_steps[what](i)

        @block.vector
        def _(dve):
            def group_sums(n):
                b = n % B
                for t in range(CT):
                    for c in range(2):
                        dve.bn_stats(ST[:, CT * b + t, c, :], X[:, b, t, c * HALF:(c + 1) * HALF]).then_inc(S["gn_bn"], 1)
                    dve.wait_ge(S["gn_bn"], 4 * n + 2 * t + 2)
                    dve.bn_aggr(MV[:, CT * b + t, :], ST[:, CT * b + t, :, :]).then_inc(S["gn_stat"], 1)

            def group_deviation(n):
                ph, b = divmod(n, B)
                cols = slice(CT * b, CT * b + CT)
                dve.wait_ge(S["gn_mu_ps"], n + 1)
                dve.tensor_copy(GM[:, cols], bank(GN_PAIR[ph][b], 0)[:, 0:CT]).then_inc(S["gn_mid"], 1)
                dve.wait_ge(S["gn_mid"], 2 * n + 1)
                dve.tensor_tensor(GV[:, cols], MV[:, cols, 0], GM[:, cols], ALU.subtract).then_inc(S["gn_dev"], 1)
                dve.wait_ge(S["gn_dev"], n + 1)
                dve.tensor_tensor(GV[:, cols], GV[:, cols], GV[:, cols], ALU.mult).then_inc(S["gn_mid"], 1)
                dve.wait_ge(S["gn_mid"], 2 * n + 2)
                dve.tensor_tensor(GV[:, cols], GV[:, cols], MV[:, cols, 1], ALU.add).then_inc(S["gn_v"], 1)

            def group_apply(n):
                ph, b = divmod(n, B)
                dve.wait_ge(S["gn_rstd"], n + 1)
                for t in range(CT):
                    i, dst = CT * b + t, (XG, XG2)[ph][:, b, t]
                    ins = dve.tensor_scalar(dst, X[:, b, t], GM[:, i:i + 1], GR[:, i:i + 1], ALU.subtract, ALU.mult)
                    if ph == 0:
                        ins.then_inc(S["gn_pre"], 1)
                        dve.wait_ge(S["gn_pre"], i + 1)
                        ins = dve.tensor_scalar(dst, dst, CLAMP, -CLAMP, ALU.min, ALU.max)
                    ins.then_inc(S["gn_out"], 1)

            def pixel_center(n):
                ph, b = divmod(n, B)
                dve.wait_ge(S["ln_mu_ps"], n + 1)
                for t in range(CT):
                    xt = (XG, XO)[ph][:, b, t]
                    dve.tensor_tensor(xt, xt, pair(MEAN_PAIR[ph][b]), ALU.subtract).then_inc(S["ln_cent"], 1)

            def pixel_scale(n):
                ph, b = divmod(n, B)
                dve.wait_ge(S["ln_rstd"], n + 1)
                for t in range(CT):
                    xt, i = (XG, XO)[ph][:, b, t], 2 * CT * n + 2 * t
                    dve.wait_ge(S["ln_cent"], CT * n + t + 1)
                    dve.tensor_tensor(xt, xt, RSO[b] if ph else RS[:, b], ALU.mult).then_inc(S["ln_self"], 1)
                    dve.wait_ge(S["ln_self"], i + 1)
                    if ph == 0:
                        dve.tensor_scalar(xt, xt, NW[:, t:t + 1], NB[:, t:t + 1], ALU.mult, ALU.add).then_inc(S["ln_self"], 1)
                        dve.wait_ge(S["ln_self"], i + 2)
                        dve.tensor_scalar(xt, xt, CLAMP, -CLAMP, ALU.min, ALU.max).then_inc(S["ln_out"], 1)
                    else:
                        dve.tensor_scalar(xt, xt, CLAMP, -CLAMP, ALU.min, ALU.max).then_inc(S["ln_self"], 1)
                        dve.wait_ge(S["ln_self"], i + 2)
                        dve.wait_ge(S["ld_x1"], 32)
                        dve.tensor_tensor(X[:, b, t], X[:, b, t], xt, ALU.add).then_inc(S["x1_rd"], 1)

            for b in range(B):
                dve.wait_ge(S[f"ld_x_b{b}"], 16)
                group_sums(b)
            dve.wait_ge(S["ld_cst"], 16)
            dve.wait_ge(S["ld_c"], 48)
            for b in range(B):
                group_deviation(b)
            for b in range(B):
                group_apply(b)
            for b in range(B):
                pixel_center(b)
            dve.wait_ge(S["ld_alr"], 16)
            dve.tensor_scalar(ALR, ALR, LOG_A_CAP, None, ALU.is_le).then_inc(S["alr_le"], 1)
            for b in range(B):
                pixel_scale(b)
            dve.wait_ge(S["a_exp"], 1)
            dve.tensor_scalar(AC[:, :], AC[:, :], -1.0, None, ALU.mult).then_inc(S["a_rd"], 1)
            for e in range(NG):
                m = e % DT_
                dve.wait_ge(S["xin_rd"], 2 * e + 2)
                for k in range(KC - 1):
                    if k:
                        dve.wait_ge(S["conv_self"], 2 * e + k)
                    ins = dve.scalar_tensor_tensor(out=CA[:, e % 2], in0=XIN[:, e % 2, k:k + L], scalar=CW[:, m, k:k + 1], in1=CA[:, e % 2], op0=ALU.mult, op1=ALU.add)
                    ins.then_inc(S["conv_out"] if k == KC - 2 else S["conv_self"], 1)

            def take_v(i):
                dve.wait_ge(S["dt_ps"], i + 1)
                if i >= 2:
                    dve.wait_ge(S["sp_abs"], i - 1)
                    dve.wait_ge(S["dt_rd"], i - 1)
                dve.tensor_scalar(VV[i % 2], pair(from_xd_pair("dt", i)), DTB[:, i % DT_:i % DT_ + 1], None, ALU.add).then_inc(S["v_rd"], 1)

            take_v(0)
            for i in range(NG + 1):
                if i >= 1:
                    e = i - 1
                    dve.wait_ge(S["sp_corr"], e + 1)
                    dve.scalar_tensor_tensor(out=DTF[:, e % 2], in0=LNB[:, e % 2], scalar=0.0, in1=DTF[:, e % 2], op0=ALU.min, op1=ALU.add).then_inc(S["sp_sum"], 1)
                    dve.wait_ge(S["sp_sum"], e + 1)
                    dve.scalar_tensor_tensor(out=DTF[:, e % 2], in0=VV[e % 2], scalar=0.0, in1=DTF[:, e % 2], op0=ALU.max, op1=ALU.add).then_inc(S["dt_rd"], 1)
                    if e >= 1:
                        dve.wait_ge(S["mid_rd"], e)
                        dve.wait_ge(S["dt_lo"], e)
                    dve.wait_ge(S["dt_rd"], e + 1)
                    dve.tensor_tensor(DTR, DTF[:, e % 2], high(DTF[:, e % 2]), ALU.subtract).then_inc(S["dt_r"], 1)
                if i < NG:
                    if i >= 1:
                        dve.wait_ge(S["sp_corr"], i)
                    dve.wait_ge(S["sp_exp"], i + 1)
                    dve.tensor_scalar(UM1[:, :], DTF[:, i % 2], 1.0, 1.0, ALU.add, ALU.subtract).then_inc(S["um1_rd"], 1)
                if i < NG - 1:
                    take_v(i + 1)
                if i >= 1:
                    if e >= 2:
                        dve.wait_ge(dt_st[e % 2], 16 * (e // 2))
                    dve.wait_ge(S["dt_r"], e + 1)
                    dve.tensor_tensor(dt_parts[:, e % 2, 2], DTR, high(DTR), ALU.subtract).then_inc(S["dt_lo"], 1)
                    dve.wait_ge(S["hi_rd"], e + 1)
                    dve.tensor_scalar(dt_parts[:, e % 2, 3], HT[:, e % 2], CAP, 0.0, ALU.subtract, ALU.max).then_inc(S["ex_lim"], 1)
                    dve.wait_ge(S["ex_lim"], e + 1)
                    dve.scalar_tensor_tensor(out=dt_parts[:, e % 2, 3], in0=HT[:, e % 2], scalar=63.0 / 64, in1=dt_parts[:, e % 2, 3],
                                             op0=ALU.mult, op1=ALU.min).then_inc(S["ex_rd"], 1)
                    dve.wait_ge(S["ex_rd"], e + 1)
                    dve.tensor_tensor(dt_parts[:, e % 2, 0], HT[:, e % 2], dt_parts[:, e % 2, 3], ALU.subtract).then_inc(S["hic_rd"], 1)

                if i in (0, 2):
                    b = i // 2
                    dve.wait_ge(S["rep_ps"], 2 * b + 1)
                    dve.tensor_copy(BR[:, b], pair(from_xd_pair("b", b))).then_inc(S["brep_rd"], 1)

            def take_u(it, b, t, first):
                dve.wait_ge(S["bc_dx"], GT * it + t + 1)
                if not first or t >= 4:
                    dve.wait_ge(S["g_rd"], GT * it + t - 3)
                dve.tensor_tensor(H[:, t % 4], pair(2), BR[:, b], ALU.mult).then_inc(S["u_rd"], 1)

            def scan(it, t):
                dve.wait_ge(S["da_rd"], GT * it + t + 1)
                dve.wait_ge(S["u_rd"], GT * it + t + 1)
                dve.tensor_tensor_scan(H[:, t % 4], pair(t % 2), H[:, t % 4], 0.0, ALU.mult, ALU.add).then_inc(S["scan_rd"], 1)

            def gate(it):
                dve.wait_ge(S["red_ps"], 4 * it + 4)
                dve.tensor_tensor(XC[:, it], pair(3), SZ[:, it], ALU.mult).then_inc(S["y_rd"], 1)

            def group(it, first):
                b = 0 if first else (it >> 2) & 1
                for t in range(GT):
                    take_u(it, b, t, first)
                    if t == 6 and first:
                        for r in range(2):
                            dve.wait_ge(dx_st[r], 16 * NG // 2)
                        dve.memset(stack[96:P, 1, 1], 0.0).then_inc(S["stk_zero1"], 1)
                    if t:
                        scan(it, t - 1)
                    elif not first:
                        scan(it - 1, GT - 1)
                    if t == 6 and not first:
                        gate(it - 1)

            dve.wait_ge(S["sz_rd"], NG)
            for used in ("hi_rd", "dt_r", "dx_rd", "dx_r", "dxhi_rd"):
                dve.wait_ge(S[used], NG)
            dve.wait_ge(S["brep_rd"], B)
            group(0, True)
            with dve.Fori(1, NG) as it:
                group(it, False)
            scan(NG - 1, GT - 1)
            gate(NG - 1)
            def clamp_output(b, t):
                dve.wait_ge(S["op_ps"], CT * b + t + 1)
                dve.tensor_scalar(XO[:, b, t], pair(OP_PAIR[b][t]), CLAMP, -CLAMP, ALU.min, ALU.max).then_inc(S["op_rd"], 1)

            dve.wait_ge(S["y_rd"], DT_)
            clamp_output(0, 0)
            clamp_output(0, 1)
            pixel_center(2)
            clamp_output(1, 0)
            pixel_scale(2)
            clamp_output(1, 1)
            dve.wait_ge(S["x1_rd"], CT)
            group_sums(2)
            pixel_center(3)
            group_deviation(2)
            group_apply(2)
            pixel_scale(3)
            dve.wait_ge(S["x1_rd"], B * CT)
            dve.memset(VT[:, :, :, P:P + 1], 1.0).then_inc(S["one_set"], 1)
            group_sums(3)
            group_deviation(3)
            group_apply(3)
            dve.wait_ge(S["bn_ln"], 2)
            dve.tensor_tensor(INV[:, :], INV[:, :], BNG, ALU.mult).then_inc(S["bn_self"], 1)
            dve.wait_ge(S["bn_self"], 1)
            dve.tensor_tensor(SHF[:, :], BNM, INV[:, :], ALU.mult).then_inc(S["bn_self"], 1)
            dve.wait_ge(S["bn_self"], 2)
            dve.tensor_tensor(SHF[:, :], BNB, SHF[:, :], ALU.subtract).then_inc(S["bn_rd"], 1)
            dve.wait_ge(S["bn_rd"], 1)

            def take_states(b):
                for w in range(4):
                    i = 4 * b + w
                    dve.wait_ge(S["vk_ps"], i + 1)
                    if b:
                        dve.wait_ge(S["nd_ps"], 16 * b)
                    dve.tensor_copy(KS[:, w:w + 1], bank(3, w % 2)[:, P:P + 1]).then_inc(S["ks_rd"], 1)
                    dve.tensor_tensor(VKS[w][:, 0, :], bank(3, w % 2)[:, 0:P], MASK, ALU.mult).then_inc(S["vks_rd"], 1)
                    dve.wait_ge(S["ks_rd"], i + 1)
                    dve.tensor_scalar(VKS[w][:, 1, :], MASK, KS[:, w:w + 1], None, ALU.mult).then_inc(S["vks_rd"], 1)

            def divide(u):
                b, i = divmod(u, 8)
                w, c = divmod(i, 2)
                dve.wait_ge(S["nd_ps"], 2 * u + 2)
                dve.wait_ge(S["den_rd"], u + 1)
                dve.tensor_tensor(QR[b][:, w, c * HALF:(c + 1) * HALF], bank(attend_pair(u), 0), den_slot(u), ALU.mult).then_inc(S["o_rd"], 1)

            def add_projected(p):
                b, i = divmod(p, 4)
                m, c = divmod(i, 2)
                half = X[:, b, m, c * HALF:(c + 1) * HALF]
                dve.wait_ge(S["pr_ps"], p + 1)
                dve.scalar_tensor_tensor(out=half, in0=bank(project_pair(p), c), scalar=INV[:, m:m + 1], in1=half, op0=ALU.mult, op1=ALU.add).then_inc(S["pr_rd"], 1)

            def dve_between(n, c):
                for what, i in between(n, c):
                    if what == "states":
                        take_states(i)
                    elif what == "attend":
                        divide(i)
                    elif what == "project":
                        add_projected(i)

            for n in range(B * QT):
                b, j = divmod(n, QT)
                t = ORDER[j]
                dve.wait_ge(S["pad_rd"], n + 1)
                for i in range(dve_taps(n)):
                    k = PE_TAPS[n] + POOL_TAPS[n] + i
                    partial = pair(1).rearrange("p (y x) -> p y x", x=HW)
                    last = i == dve_taps(n) - 1
                    if i == 0:
                        dve.wait_ge(S["pool_add"], pool_adds(n + 1))
                        if n:
                            dve.wait_ge(S["acc_rd"], n)
                    else:
                        dve.wait_ge(S["acc_self"], dve_partials(n) + i)
                    if last and n >= 2:
                        dve.wait_ge(S["cv_ps"], 2 * n - 2)
                    ins = dve.scalar_tensor_tensor(out=ACC[:, n % 2] if last else partial, in0=tap(b, t, k), scalar=DW[:, t, k:k + 1],
                                                   in1=partial if i else POOL_SUMS[n % 2], op0=ALU.mult, op1=ALU.add)
                    ins.then_inc(S["acc_rd"] if last else S["acc_self"], 1)
                    if n and i in (dve_taps(n) // 3, dve_taps(n) - 2):
                        dve_between(n - 1, 0 if i == dve_taps(n) // 3 else 1)
                    if n < B * CT and i == 3:
                        k = divmod(n, CT)
                        dve.tensor_scalar(X[:, k[0], k[1]], X[:, k[0], k[1]], SHF[:, k[1]:k[1] + 1], None, ALU.add).then_inc(S["bn_rd"], 1)
            dve.wait_ge(S["bn_rd"], 1 + B * CT)
            for c in range(2):
                dve_between(B * QT - 1, c)


def constants():
    import numpy as np
    p = np.arange(P)
    same_head = (p[:, None] // HD == p[None, :] // HD).astype(np.float32)
    cst = np.zeros((P, 6, P), np.float32)
    cst[:, 0] = same_head / HD
    cst[:, 1] = 1.0 / C
    cst[:, 2] = np.eye(P, dtype=np.float32)
    for n in range(NS):
        cst[R + n, 3, n::NS] = 1.0
        cst[R + NS + n, 4, n::NS] = 1.0
    cst[:, 5] = same_head
    selr = np.zeros((P, 4, 32), np.float32)
    selb = np.zeros((P, 4, P), np.float32)
    for j in range(4):
        for d in range(OCT):
            selr[d * NS:(d + 1) * NS, j, OCT * j + d] = 1.0
            for i in range(PARTS + 1):
                selb[32 * i + OCT * j + d, j, d * NS:(d + 1) * NS] = 1.0
    return cst, selr, selb


def kernel(**inputs):
    import numpy as _np
    import concourse.bacc as _bacc
    from concourse import mybir as _mybir
    from concourse.bass_utils import run_bass_kernel_spmd as _run

    v = {n.replace("L0_conv_", "a_").replace("L1_conv_", "b_"): _np.asarray(t) for n, t in inputs.items()}
    by_tile = lambda t: t.reshape(-1, P).T
    by_role = lambda t: t.reshape(C // HD, 3, HD, -1).swapaxes(0, 1).reshape(QC, -1)
    cst, selr, selb = constants()
    cols = _np.concatenate([
        by_tile(v["a_norm_w"]), by_tile(v["a_norm_b"]),
        v["a_conv_w"].reshape(DT_, P, KC).swapaxes(0, 1).reshape(P, DT_ * KC),
        by_tile(v["a_conv_b"]), by_tile(v["a_dt_proj_b"]), by_tile(v["a_D"]),
        by_tile(v["b_bn_gamma"]), by_tile(v["b_bn_beta"]), by_tile(v["b_bn_mean"]), by_tile(v["b_bn_var"])], axis=1)
    laid = {
        "x": v["x"].reshape(B, C, L),
        "win": v["a_in_proj_w"].T, "xpw": v["a_x_proj_w"].T, "dtw": v["a_dt_proj_w"].T,
        "alogr": v["a_A_log"], "alog": v["a_A_log"].reshape(DI // OCT, P).T, "wout": v["a_out_proj_w"].T,
        "wq": by_role(v["b_qkv_w"]).T, "wpr": v["b_proj_w"].T,
        "dw": by_role(v["b_dw_w"]),
        "pw": v["b_pw_w"].reshape(C // HD, 3, HD, HD).transpose(1, 0, 3, 2).reshape(QC, HD),
        "cols": cols, "cst": cst, "selr": selr, "selb": selb.astype(_mybir.dt.np(BF16)),
    }
    nc = _bacc.Bacc("TRN2", target_bir_lowering=False, num_devices=1)
    arrays, args = {}, {}
    for name, t in laid.items():
        t = _np.ascontiguousarray(t)
        arrays[f"in_{name}"] = t
        args[name] = nc.dram_tensor(f"in_{name}", t.shape, _mybir.dt.from_np(t.dtype), kind="ExternalInput").ap()
    out = nc.dram_tensor("out_0", (B, C, L), F32, kind="ExternalOutput").ap()
    mamba_attention_kernel(nc, args, out)
    r = _run(nc, [arrays], core_ids=[0])
    return r.results[0]["out_0"].reshape(B, C, HW, HW)
```
